# Optimizing a Trainium2 kernel written in Bass

```python
import numpy as np
import jax
import jax.numpy as jnp

def _softmax(x, axis=-1):
    return jax.nn.softmax(x, axis=axis)

def _gelu(x):
    return jax.nn.gelu(x, approximate=True)

def _silu(x):
    return jax.nn.silu(x)

def _sigmoid(x):
    return jax.nn.sigmoid(x)

def _layernorm(x, axis=-1, eps=1e-05):
    m = jnp.mean(x, axis=axis, keepdims=True)
    v = jnp.var(x, axis=axis, keepdims=True)
    return (x - m) / jnp.sqrt(v + eps)

def _scatter_add(tgt, idx, src, axis=0):
    return tgt.at[idx].add(src)

def _segment_sum(src, seg, n):
    return jax.ops.segment_sum(src, seg, n)
kernel_name = 'mk_metaformer_d1_conv_nchw512_r4_ecfa96'

def setup_inputs(seed: int=0):
    np.random.seed(seed)
    _w = jnp.asarray

    def _rec_inputs():
        import jax
        import jax.numpy as jnp
        _gk = jax.random.key(seed)
        x = 7.22e-05 + 1 * jax.random.normal(jax.random.fold_in(_gk, 1), (4, 128, 16, 16), jnp.float32)
        return x
    x = _rec_inputs()

    def _L0_conv_setup():
        import jax, jax.numpy as jnp
        from jax import lax
        import numpy as np
        INPUT_DIM = 128
        OUTPUT_DIM = 128
        D_STATE = 16
        D_CONV = 4
        EXPAND = 2
        D_MODEL = INPUT_DIM // 4
        D_INNER = EXPAND * D_MODEL
        DT_RANK = (D_MODEL + 15) // 16
        EPS = 1e-05

        def layer_norm(x, g, b):
            mu = jnp.mean(x, axis=-1, keepdims=True)
            var = jnp.mean((x - mu) ** 2, axis=-1, keepdims=True)
            return (x - mu) * lax.rsqrt(var + EPS) * g + b

        def mamba(x, in_proj_w, conv_w, conv_b, x_proj_w, dt_proj_w, dt_proj_b, A_log, D_param, out_proj_w):
            Beff, L, _ = x.shape
            xz = jnp.einsum('bld,ed->ble', x, in_proj_w)
            xi, z = jnp.split(xz, 2, axis=-1)
            xc = lax.conv_general_dilated(xi.transpose(0, 2, 1), conv_w[:, None, :], (1,), [(D_CONV - 1, 0)], feature_group_count=D_INNER)
            xc = jax.nn.silu(xc + conv_b[None, :, None]).transpose(0, 2, 1)
            dbc = jnp.einsum('bld,ed->ble', xc, x_proj_w)
            dt = dbc[..., :DT_RANK]
            Bs = dbc[..., DT_RANK:DT_RANK + D_STATE]
            Cs = dbc[..., DT_RANK + D_STATE:]
            dt = jax.nn.softplus(jnp.einsum('blr,er->ble', dt, dt_proj_w) + dt_proj_b)
            A = -jnp.exp(A_log)

            def step(h, inp):
                dt_t, B_t, C_t, x_t = inp
                dA = jnp.exp(dt_t[:, :, None] * A)
                h = dA * h + (dt_t * x_t)[:, :, None] * B_t[:, None, :]
                y = jnp.einsum('bds,bs->bd', h, C_t)
                return (h, y)
            h0 = jnp.zeros((Beff, D_INNER, D_STATE), x.dtype)
            _, ys = lax.scan(step, h0, (dt.transpose(1, 0, 2), Bs.transpose(1, 0, 2), Cs.transpose(1, 0, 2), xc.transpose(1, 0, 2)))
            y = ys.transpose(1, 0, 2) + xc * D_param
            y = y * jax.nn.silu(z)
            return jnp.einsum('bld,od->blo', y, out_proj_w)
        key = jax.random.key(seed)
        ks = jax.random.split(key, 10)
        inp = {'x': jax.random.normal(ks[0], (4, INPUT_DIM, 16, 16), jnp.float32), 'norm_g': jnp.ones((INPUT_DIM,), jnp.float32), 'norm_b': jnp.zeros((INPUT_DIM,), jnp.float32), 'in_proj_w': jax.random.normal(ks[1], (2 * D_INNER, D_MODEL), jnp.float32) * 0.02, 'conv_w': jax.random.normal(ks[2], (D_INNER, D_CONV), jnp.float32) * 0.2, 'conv_b': jnp.zeros((D_INNER,), jnp.float32), 'x_proj_w': jax.random.normal(ks[3], (DT_RANK + 2 * D_STATE, D_INNER), jnp.float32) * 0.02, 'dt_proj_w': jax.random.normal(ks[4], (D_INNER, DT_RANK), jnp.float32) * 0.1, 'dt_proj_b': jnp.full((D_INNER,), -2.0, jnp.float32), 'A_log': jnp.log(jnp.broadcast_to(jnp.arange(1, D_STATE + 1, dtype=jnp.float32), (D_INNER, D_STATE))), 'D_param': jnp.ones((D_INNER,), jnp.float32), 'out_proj_w': jax.random.normal(ks[5], (D_MODEL, D_INNER), jnp.float32) * 0.02, 'proj_w': jax.random.normal(ks[6], (OUTPUT_DIM, INPUT_DIM), jnp.float32) * 0.02, 'proj_b': jnp.zeros((OUTPUT_DIM,), jnp.float32), 'skip_scale': jnp.ones((1,), jnp.float32)}
        return inp
    _L0_conv_all = _L0_conv_setup()
    _L0_conv_in = {k: v for k, v in _L0_conv_all.items() if k in ('norm_g', 'norm_b', 'in_proj_w', 'conv_w', 'conv_b', 'x_proj_w', 'dt_proj_w', 'dt_proj_b', 'A_log', 'D_param', 'out_proj_w', 'proj_w', 'proj_b', 'skip_scale')}
    del _L0_conv_all

    def _L0_ffn_setup():
        import jax, jax.numpy as jnp
        import numpy as np
        B, S, H, E, F, TOP_K = (4, 512, 128, 16, 256, 2)

        def _moe_forward(inputs, router_w, gate_w, up_w, down_w):
            b, s, h = inputs.shape
            x = inputs.reshape(-1, h)
            T = x.shape[0]
            router_logits = x @ router_w.T
            top_vals, top_idx = jax.lax.top_k(router_logits, TOP_K)
            weights = jax.nn.softmax(top_vals.astype(jnp.float32), axis=-1)
            combine = jnp.zeros((T, router_w.shape[0]), jnp.float32)
            combine = combine.at[jnp.arange(T)[:, None], top_idx].set(weights)

            def step(acc, ew):
                wg, wu, wd, ce = ew
                hid = jax.nn.silu(x @ wg) * (x @ wu)
                y = hid @ wd
                return (acc + ce[:, None] * y, None)
            out0 = jnp.zeros_like(x)
            out, _ = jax.lax.scan(step, out0, (gate_w, up_w, down_w, combine.T))
            return (out.reshape(b, s, h), router_logits, top_idx)
        key = jax.random.key(seed)
        k0, k1, k2, k3, k4 = jax.random.split(key, 5)
        scale = 0.02
        return {'inputs': jax.random.normal(k0, (B, S, H), dtype=jnp.float32), 'router_w': jax.random.normal(k1, (E, H), dtype=jnp.float32) * scale, 'gate_w': jax.random.normal(k2, (E, H, F), dtype=jnp.float32) * scale, 'up_w': jax.random.normal(k3, (E, H, F), dtype=jnp.float32) * scale, 'down_w': jax.random.normal(k4, (E, F, H), dtype=jnp.float32) * scale}
    _L0_ffn_all = _L0_ffn_setup()
    _L0_ffn_in = {k: v for k, v in _L0_ffn_all.items() if k in ('router_w', 'gate_w', 'up_w', 'down_w')}
    del _L0_ffn_all
    return {'x': x, 'L0_conv_norm_g': _L0_conv_in['norm_g'], 'L0_conv_norm_b': _L0_conv_in['norm_b'], 'L0_conv_in_proj_w': _L0_conv_in['in_proj_w'], 'L0_conv_conv_w': _L0_conv_in['conv_w'], 'L0_conv_conv_b': _L0_conv_in['conv_b'], 'L0_conv_x_proj_w': _L0_conv_in['x_proj_w'], 'L0_conv_dt_proj_w': _L0_conv_in['dt_proj_w'], 'L0_conv_dt_proj_b': _L0_conv_in['dt_proj_b'], 'L0_conv_A_log': _L0_conv_in['A_log'], 'L0_conv_D_param': _L0_conv_in['D_param'], 'L0_conv_out_proj_w': _L0_conv_in['out_proj_w'], 'L0_conv_proj_w': _L0_conv_in['proj_w'], 'L0_conv_proj_b': _L0_conv_in['proj_b'], 'L0_conv_skip_scale': _L0_conv_in['skip_scale'], 'L0_ffn_router_w': _L0_ffn_in['router_w'], 'L0_ffn_gate_w': _L0_ffn_in['gate_w'], 'L0_ffn_up_w': _L0_ffn_in['up_w'], 'L0_ffn_down_w': _L0_ffn_in['down_w']}

def reference(x, L0_conv_norm_g, L0_conv_norm_b, L0_conv_in_proj_w, L0_conv_conv_w, L0_conv_conv_b, L0_conv_x_proj_w, L0_conv_dt_proj_w, L0_conv_dt_proj_b, L0_conv_A_log, L0_conv_D_param, L0_conv_out_proj_w, L0_conv_proj_w, L0_conv_proj_b, L0_conv_skip_scale, L0_ffn_router_w, L0_ffn_gate_w, L0_ffn_up_w, L0_ffn_down_w):
    import jax
    import jax.numpy as jnp

    def _L0_conv_ref(x, norm_g, norm_b, in_proj_w, conv_w, conv_b, x_proj_w, dt_proj_w, dt_proj_b, A_log, D_param, out_proj_w, proj_w, proj_b, skip_scale):
        import jax, jax.numpy as jnp
        from jax import lax
        import numpy as np
        INPUT_DIM = 128
        OUTPUT_DIM = 128
        D_STATE = 16
        D_CONV = 4
        EXPAND = 2
        D_MODEL = INPUT_DIM // 4
        D_INNER = EXPAND * D_MODEL
        DT_RANK = (D_MODEL + 15) // 16
        EPS = 1e-05

        def layer_norm(x, g, b):
            mu = jnp.mean(x, axis=-1, keepdims=True)
            var = jnp.mean((x - mu) ** 2, axis=-1, keepdims=True)
            return (x - mu) * lax.rsqrt(var + EPS) * g + b

        def mamba(x, in_proj_w, conv_w, conv_b, x_proj_w, dt_proj_w, dt_proj_b, A_log, D_param, out_proj_w):
            Beff, L, _ = x.shape
            xz = jnp.einsum('bld,ed->ble', x, in_proj_w)
            xi, z = jnp.split(xz, 2, axis=-1)
            xc = lax.conv_general_dilated(xi.transpose(0, 2, 1), conv_w[:, None, :], (1,), [(D_CONV - 1, 0)], feature_group_count=D_INNER)
            xc = jax.nn.silu(xc + conv_b[None, :, None]).transpose(0, 2, 1)
            dbc = jnp.einsum('bld,ed->ble', xc, x_proj_w)
            dt = dbc[..., :DT_RANK]
            Bs = dbc[..., DT_RANK:DT_RANK + D_STATE]
            Cs = dbc[..., DT_RANK + D_STATE:]
            dt = jax.nn.softplus(jnp.einsum('blr,er->ble', dt, dt_proj_w) + dt_proj_b)
            A = -jnp.exp(A_log)

            def step(h, inp):
                dt_t, B_t, C_t, x_t = inp
                dA = jnp.exp(dt_t[:, :, None] * A)
                h = dA * h + (dt_t * x_t)[:, :, None] * B_t[:, None, :]
                y = jnp.einsum('bds,bs->bd', h, C_t)
                return (h, y)
            h0 = jnp.zeros((Beff, D_INNER, D_STATE), x.dtype)
            _, ys = lax.scan(step, h0, (dt.transpose(1, 0, 2), Bs.transpose(1, 0, 2), Cs.transpose(1, 0, 2), xc.transpose(1, 0, 2)))
            y = ys.transpose(1, 0, 2) + xc * D_param
            y = y * jax.nn.silu(z)
            return jnp.einsum('bld,od->blo', y, out_proj_w)
        B, C, H, W = x.shape
        L = H * W
        xf = x.reshape(B, C, L).transpose(0, 2, 1)
        xn = layer_norm(xf, norm_g, norm_b)
        chunks = xn.reshape(B, L, 4, D_MODEL).transpose(2, 0, 1, 3).reshape(4 * B, L, D_MODEL)
        ym = mamba(chunks, in_proj_w, conv_w, conv_b, x_proj_w, dt_proj_w, dt_proj_b, A_log, D_param, out_proj_w)
        ym = ym + skip_scale * chunks
        y = ym.reshape(4, B, L, D_MODEL).transpose(1, 2, 0, 3).reshape(B, L, C)
        y = layer_norm(y, norm_g, norm_b)
        y = jnp.einsum('blc,oc->blo', y, proj_w) + proj_b
        return y.transpose(0, 2, 1).reshape(B, OUTPUT_DIM, H, W)

    def _L0_ffn_ref(inputs, router_w, gate_w, up_w, down_w):
        import jax, jax.numpy as jnp
        import numpy as np
        B, S, H, E, F, TOP_K = (4, 512, 128, 16, 256, 2)

        def _moe_forward(inputs, router_w, gate_w, up_w, down_w):
            b, s, h = inputs.shape
            x = inputs.reshape(-1, h)
            T = x.shape[0]
            router_logits = x @ router_w.T
            top_vals, top_idx = jax.lax.top_k(router_logits, TOP_K)
            weights = jax.nn.softmax(top_vals.astype(jnp.float32), axis=-1)
            combine = jnp.zeros((T, router_w.shape[0]), jnp.float32)
            combine = combine.at[jnp.arange(T)[:, None], top_idx].set(weights)

            def step(acc, ew):
                wg, wu, wd, ce = ew
                hid = jax.nn.silu(x @ wg) * (x @ wu)
                y = hid @ wd
                return (acc + ce[:, None] * y, None)
            out0 = jnp.zeros_like(x)
            out, _ = jax.lax.scan(step, out0, (gate_w, up_w, down_w, combine.T))
            return (out.reshape(b, s, h), router_logits, top_idx)
        out, router_logits, selected_experts = _moe_forward(inputs, router_w, gate_w, up_w, down_w)
        return out

    def _gn(v, G=32, eps=1e-05):
        B_, C_, H_, W_ = v.shape
        g = v.reshape(B_, G, C_ // G, H_, W_)
        m = jnp.mean(g, axis=(2, 3, 4), keepdims=True)
        s = jnp.var(g, axis=(2, 3, 4), keepdims=True)
        return ((g - m) / jnp.sqrt(s + eps)).reshape(v.shape)

    def _ln_c(v, eps=1e-06):
        m = jnp.mean(v, axis=1, keepdims=True)
        s = jnp.var(v, axis=1, keepdims=True)
        return (v - m) / jnp.sqrt(s + eps)

    def _ln_t(v, eps=1e-05):
        m = jnp.mean(v, axis=-1, keepdims=True)
        s = jnp.var(v, axis=-1, keepdims=True)
        return (v - m) / jnp.sqrt(s + eps)

    def _to_tokens(v):
        B_, C_, H_, W_ = v.shape
        return v.reshape(B_, C_, H_ * W_).transpose(0, 2, 1)

    def _from_tokens(t, like):
        B_, C_, H_, W_ = like.shape
        return t.transpose(0, 2, 1).reshape(B_, C_, H_, W_)
    x = x + _L0_conv_ref(_ln_c(x), L0_conv_norm_g, L0_conv_norm_b, L0_conv_in_proj_w, L0_conv_conv_w, L0_conv_conv_b, L0_conv_x_proj_w, L0_conv_dt_proj_w, L0_conv_dt_proj_b, L0_conv_A_log, L0_conv_D_param, L0_conv_out_proj_w, L0_conv_proj_w, L0_conv_proj_b, L0_conv_skip_scale)
    t = _to_tokens(x)
    t = t + _L0_ffn_ref(_ln_t(t), L0_ffn_router_w, L0_ffn_gate_w, L0_ffn_up_w, L0_ffn_down_w)
    x = _from_tokens(t, x)
    return x

_drawn_inputs = setup_inputs


def setup_inputs(seed=0):
    import zlib

    import numpy as np

    out = dict(_drawn_inputs(seed))
    spreads = {'L0_conv_norm_g': (1.0, 0.2),
     'L0_conv_norm_b': (0.0, 0.1),
     'L0_conv_conv_b': (0.0, 0.8),
     'L0_conv_dt_proj_b': (-2.0, 0.6),
     'L0_conv_D_param': (1.0, 0.6),
     'L0_conv_proj_b': (0.0, 0.1)}
    factors = {'L0_conv_in_proj_w': 8.0,
     'L0_conv_conv_w': 8.0,
     'L0_conv_x_proj_w': 8.0,
     'L0_conv_dt_proj_w': 8.0,
     'L0_conv_A_log': 8.0,
     'L0_conv_out_proj_w': 8.0,
     'L0_ffn_router_w': 8.0,
     'L0_ffn_gate_w': 8.0,
     'L0_ffn_up_w': 8.0,
     'L0_ffn_down_w': 8.0}
    for name, (base, spread) in spreads.items():
        noise = np.random.default_rng([zlib.crc32(name.encode()), seed]).standard_normal(out[name].shape)
        drawn = base * np.exp(spread * noise) if base else spread * noise
        out[name] = jnp.asarray(drawn.astype(out[name].dtype))
    for name, factor in factors.items():
        out[name] = (out[name] * factor).astype(out[name].dtype)
    return out
```

```python
from contextlib import ExitStack

import numpy as np
import concourse.bass as bass
from concourse import mybir

P = 128
BATCH, C, T = 4, 128, 256
CHUNKS, DM, DI = 4, 32, 64
PAIRS = CHUNKS // 2
NS = 16
RANK = 2
TAPS = 4
E, F = 16, 256
FH = F // P
HALVES = 2
N = BATCH * T // HALVES
GROUPS = HALVES * PAIRS
DTK = 2 * RANK + 1
LN2 = float(np.log(2.0))
LOG1P = (2.00000001, 0.66666317, 0.40024839, 0.27961494, 0.28174741)
BLK = N // P
EPS_IN, EPS = 1e-6, 1e-5
WCH = 2
CHUNKS_W = 2 * E // WCH
SCAN0, SCAN1 = 0, PAIRS * NS
STEPS = GROUPS * NS
POOL0 = 3 * NS
POOL_SLOTS = 20
FRONT_W = 8
PIECES = 9

F32, F32R, U32 = mybir.dt.float32, mybir.dt.float32r, mybir.dt.uint32
ALU, ACT = mybir.AluOpType, mybir.ActivationFunctionType

COLS = {}
_at = 0
for _name, _width in (("norm_g", 1), ("norm_b", 1), ("proj_b", 1), ("skip", 1), ("conv_w", TAPS), ("conv_b", 1),
                      ("D", 1), ("A_log", NS), ("in_x", P), ("in_z", P), ("bc", P), ("dt_in", 2 * RANK),
                      ("dt_out", P), ("out", 2 * DM), ("proj", P), ("router", E)):
    COLS[_name] = (_at, _at + _width)
    _at += _width
NPACK = _at


def build(nc, x, params, gate_w, up_w, down_w, out):
    with ExitStack() as ctx:
        def sb(name, shape, dt=F32):
            return ctx.enter_context(nc.sbuf_tensor(name, shape, dt))

        bank = [ctx.enter_context(nc.psum_tensor(f"bank{i}", [P, N], F32)) for i in range(8)]
        DECAY = (0, 1)
        STATE_SUM = (7, 6, 7)
        BACK = ((4, 5, 6), (0, 1, 2))
        YSUM, SPREAD = 6, 7

        B_BANK = 2

        def c_bank(k):
            return 3 + k % 3 if k < SCAN1 else 3

        def c_before(k):
            return max((j + 1 for j in range(k) if c_bank(j) == c_bank(k)), default=0)

        def gate_bank(k, f):
            return 0 if k >= E and f else 4

        def up_bank(k, f):
            return 1 if k >= E and f else 5

        X = sb("X", [P, HALVES, N])
        par = sb("par", [P, NPACK])
        W_hi = [sb("Wg_hi", [P, E, F], F32R), sb("Wu_hi", [P, E, F], F32R)]
        W_lo = [sb("Wg_lo", [P, E, F], F32R), sb("Wu_lo", [P, E, F], F32R)]
        Wd = sb("Wd", [P, E, FH, C])
        mean_w = sb("mean_w", [P, P])
        var_in_w = sb("var_in_w", [P, P])
        cst = sb("cst", [P, 4])
        ident = sb("ident", [P, P])
        iota_e = sb("iota_e", [P, BLK, E])
        sel = sb("sel", [P, NS, P], F32R)
        sel_e = sb("sel_e", [P // 2, E, P], F32R)
        A = sb("A", [P, NS])
        xm = sb("xm", [P, HALVES, N])
        sq = sb("sq", [P, HALVES, N])
        chk = sb("chk", [P, HALVES, N])
        xc = sb("xc", [P, GROUPS, N])
        zs = sb("zs", [P, GROUPS, N])
        dt = sb("dt", [P, GROUPS, N])
        dtx = sb("dtx", [P, GROUPS, N])
        BC = sb("BC", [P, GROUPS, N], F32R)
        y = sb("y", [P, GROUPS, N])
        ring = sb("ring", [P, 3 + 2 + 2 + 3, N])
        u, Bs, h, hc = ring[:, 0:3], ring[:, 3:5], ring[:, 5:7], ring[:, 7:10]
        L = sb("L", [P, BLK, E])
        top = sb("top", [P, BLK, 8])
        topi = sb("topi", [P, BLK, 8], U32)
        topf = sb("topf", [P, BLK, 2])
        w01 = sb("w01", [P, BLK, 2])
        e1 = sb("e1", [P, BLK, 1])
        oh = sb("oh", [P, 2, BLK, E])
        cpad = sb("cpad", [P, BLK, P // 2])
        CE = sb("CE", [P // 2, HALVES, N], F32R)
        tn_hi = sb("tn_hi", [P, HALVES, N], F32R)
        tn_lo = sb("tn_lo", [P, HALVES, N], F32R)
        xs_hi = sb("xs_hi", [P, 2, N], F32R)
        xs_lo = sb("xs_lo", [P, 2, N], F32R)
        xs = xc[:, 0, :]
        th = dt[:, 0:FH]
        hid = (y[:, 0:FH], zs[:, 0:FH])
        tn = xm
        dtr = ring[0:DTK, 5:5 + GROUPS]
        lr = ring[:, 0:GROUPS]
        lw = dtx
        sel_tmp = y[:].rearrange("p g n -> p (g n)")
        sel_e_tmp = dt[0:64].rearrange("p g n -> p (g n)")
        stage = (sq[:, 0], sq[:, 1])

        eps_in, eps, zero, mln2 = (cst[:, i:i + 1] for i in range(4))

        def p(name):
            a, b = COLS[name]
            return par[:, a:b]

        names = ("x_in0 x_in1 par_in wd_in const0 const1 ident_r sel0 sel1 sel_r sele_r A_r cen_r sq_r mean_r var_r ln_r "
                 "rstd_r norm_r chk_r xi_r z_r conv_r xc_r zs_r bc_r dtraw_r dtr_r dtp_r bch_r bcl_r abs_r lz_r lw_r "
                 "lq_r lp_r dt_r dtx_r pB pC Bs_r dA_r u_r scan_r hc_r red_r acc_r yg_r y_r op_r y2_r y3_r "
                 "pj_r x1_r tn_r tnh_r tnl_r lg_r L_r top_r topi_r topf_r dif_r ex_r sum_r w0_r w1_r eq_r ow_r ce_r "
                 "tr_r ceh_r cel_r ceb_r xs_r xsh_r xsl_r g_r up_r th_r m_r hid_r yd_r res_r out_d "
                 "w_hi w_lo").split() + [f"w_in{c}" for c in range(CHUNKS_W)]
        S = {n: ctx.enter_context(nc.semaphore(n)) for n in names}

        def acc_count(k):
            return sum(1 for i in range(POOL0, k) if i % NS)

        def beside(slot):
            steps = [i for i in range(POOL_SLOTS) if i % 5 != 4]
            if slot in steps:
                return POOL0 + steps.index(slot)
            return STEPS if slot == POOL_SLOTS else None

        def back_pieces(e):
            first = POOL_SLOTS // FH + 1
            i, room = e - first, E - first
            return range(PIECES * i // room, PIECES * (i + 1) // room) if i >= 0 else ()

        block = ctx.enter_context(nc.Block())

        @block.sync
        def _(sp):
            for hb in range(HALVES):
                sp.dma_start(X[:, hb, :].rearrange("p (b t) -> p b t", t=T),
                             x[2 * hb:2 * hb + 2].rearrange("b c t -> c b t")).then_inc(S[f"x_in{hb}"], 16)
            for c in range(CHUNKS_W):
                if c >= 2:
                    sp.wait_ge(S["w_lo"], c - 1)
                else:
                    sp.wait_ge(S["norm_r"], c + 1)
                src = (gate_w, up_w)[c * WCH // E][c * WCH % E:c * WCH % E + WCH]
                sp.dma_start(stage[c % 2].rearrange("p (e f) -> p e f", f=F), src.rearrange("e h f -> h e f"))\
                    .then_inc(S[f"w_in{c}"], 16)
                if c == 3:
                    sp.dma_start(Wd[:], down_w.rearrange("e (f p) h -> p e f h", p=P)).then_inc(S["wd_in"], 16)
            for hb in range(HALVES):
                sp.wait_ge(S["res_r"], hb + 1)
                sp.dma_start(out[2 * hb:2 * hb + 2].rearrange("b c t -> c b t"),
                             X[:, hb, :].rearrange("p (b t) -> p b t", t=T)).then_inc(S["out_d"], 16)
            sp.wait_ge(S["out_d"], 16 * HALVES)

        @block.gpsimd
        def _(pool):
            g = nc.gpsimd
            g.memset(mean_w[:], 1.0 / C).then_inc(S["const0"], 1)
            g.memset(var_in_w[:], (1.0 + EPS) / C).then_inc(S["const0"], 1)
            for i, value in enumerate((EPS_IN * EPS, EPS, 0.0, -LN2)):
                g.memset(cst[:, i:i + 1], value).then_inc(S["const0"], 1)
            g.memset(sel_tmp, 0.0).then_inc(S["sel0"], 1)
            pool.wait_ge(S["sel0"], 1)
            for q in range(4):
                v = sel_tmp[32 * q:32 * q + 32, :].rearrange("r (s j d) -> r s j d", s=NS, j=2)
                g.affine_select(out=v, in_=v, compare_op=ALU.not_equal, fill=1.0, base=0,
                                pattern=[[-1, NS], [-NS, 2], [0, DI]], channel_multiplier=1).then_inc(S["sel1"], 1)
            pool.wait_ge(S["sel1"], 4)
            g.memset(dtr, 1.0).then_inc(S["const1"], 1)
            g.memset(cpad[:], 0.0).then_inc(S["const1"], 1)
            g.iota(iota_e[:], pattern=[[0, BLK], [1, E]], base=0, channel_multiplier=0,
                   allow_small_or_imprecise_dtypes=True).then_inc(S["const1"], 1)
            g.memset(ident[:], 0.0).then_inc(S["sel0"], 1)
            pool.wait_ge(S["sel0"], 2)
            g.affine_select(out=ident[:], in_=ident[:], compare_op=ALU.not_equal, fill=1.0, base=0,
                            pattern=[[-1, P]], channel_multiplier=1).then_inc(S["ident_r"], 1)
            g.memset(sel_e_tmp, 0.0).then_inc(S["sel0"], 1)
            pool.wait_ge(S["sel0"], 3)
            for part in range(2):
                v = sel_e_tmp[32 * part:32 * part + E, :].rearrange("r (e m) -> r e m", e=E)
                g.affine_select(out=v, in_=v, compare_op=ALU.not_equal, fill=0.5, base=0,
                                pattern=[[-1, E], [0, P]], channel_multiplier=1).then_inc(S["sel1"], 1)

            pool.wait_ge(S["sel1"], 6)

            def split_rest(c):
                pool.wait_ge(S["w_hi"], c + 1)
                w, es = c * WCH // E, slice(c * WCH % E, c * WCH % E + WCH)
                g.tensor_tensor(W_lo[w][:, es], stage[c % 2].rearrange("p (e f) -> p e f", f=F),
                                W_hi[w][:, es].bitcast(F32), ALU.subtract).then_inc(S["w_lo"], 1)

            for c in range(FRONT_W):
                split_rest(c)
            for gr in range(GROUPS):
                pool.wait_ge(S["dt_r"], gr + 1)
                g.tensor_tensor(dtx[:, gr, :], dt[:, gr, :], xc[:, gr, :], ALU.mult).then_inc(S["dtx_r"], 1)

            def scan_input(k):
                pool.wait_ge(S["Bs_r"], k + 1)
                if k >= 3:
                    pool.wait_ge(S["scan_r"], 2 * (k - 2))
                g.tensor_tensor(u[:, k % 3], dtx[:, k // NS, :], Bs[:, k % 2], ALU.mult).then_inc(S["u_r"], 1)

            def add_state(k):
                if k > POOL0:
                    pool.wait_ge(S["hc_r"], k + 1)
                    pool.wait_ge(S["acc_r"], acc_count(k))
                    g.tensor_tensor(y[:, k // NS, :], y[:, k // NS, :], hc[:, k % 3], ALU.add).then_inc(S["acc_r"], 1)

            def split_scaled(k):
                pool.wait_ge(S["xsh_r"], k + 1)
                if k >= 2:
                    pool.wait_ge(S["up_r"], FH * (k - 1))
                g.tensor_tensor(xs_lo[:, k % 2, :], xs, xs_hi[:, k % 2, :].bitcast(F32), ALU.subtract)\
                    .then_inc(S["xsl_r"], 1)

            pool.wait_ge(S["dtx_r"], GROUPS)
            for k in range(SCAN0, POOL0):
                scan_input(k)
                if k >= 4 and k % 2 == 0 and FRONT_W + k // 2 - 2 < CHUNKS_W:
                    split_rest(FRONT_W + k // 2 - 2)
            scan_input(POOL0)
            split_scaled(0)
            for slot in range(FH * E):
                k = beside(slot)
                if k is not None:
                    if k + 1 < STEPS:
                        scan_input(k + 1)
                    add_state(k - 1)
                if slot % FH == 0 and slot // FH + 1 < E:
                    split_scaled(slot // FH + 1)
            for e in range(E):
                split_scaled(E + e)

        @block.scalar
        def _(act):
            a = nc.scalar
            act.dma_start(par[:], params).then_inc(S["par_in"], 16)
            a.preload_act_table_set("natural_log_exp_and_others")
            act.wait_ge(S["par_in"], 16)
            act.wait_ge(S["const0"], 6)
            a.activation(A[:], p("A_log"), ACT.Exp, bias=zero).then_inc(S["A_r"], 1)

            def square(hb, n):
                act.wait_ge(S["cen_r"], n + 1)
                a.activation(sq[:, hb, :], xm[:, hb, :], ACT.Square, bias=zero).then_inc(S["sq_r"], 1)

            def inverse_std(hb, n, b, bias):
                act.wait_ge(S["var_r"], n + 1)
                a.activation(sq[:, hb, :], bank[b][:], ACT.Ln, bias=bias).then_inc(S["ln_r"], 1)
                act.wait_ge(S["ln_r"], n + 1)
                a.activation(sq[:, hb, :], sq[:, hb, :], ACT.Exp, scale=-0.5, bias=zero).then_inc(S["rstd_r"], 1)

            def round_weights(c):
                act.wait_ge(S[f"w_in{c}"], 16)
                w, es = c * WCH // E, slice(c * WCH % E, c * WCH % E + WCH)
                a.activation(W_hi[w][:, es], stage[c % 2].rearrange("p (e f) -> p e f", f=F), ACT.Copy)\
                    .then_inc(S["w_hi"], 1)

            for hb in range(HALVES):
                square(hb, hb)
            for hb in range(HALVES):
                inverse_std(hb, hb, 2 + hb, eps_in)
            a.preload_act_table_set("silu_and_others")
            for gr in range(GROUPS):
                act.wait_ge(S["z_r"], gr + 1)
                a.activation(zs[:, gr, :], bank[gr][:], ACT.Silu, bias=zero).then_inc(S["zs_r"], 1)
            for gr in range(GROUPS):
                act.wait_ge(S["conv_r"], TAPS * GROUPS - GROUPS + gr + 1)
                a.activation(xc[:, gr, :], y[:, gr, :], ACT.Silu, bias=p("conv_b")).then_inc(S["xc_r"], 1)
            a.preload_act_table_set("sigmoid_and_others")
            act.wait_ge(S["const1"], 3)
            for gr in range(GROUPS):
                act.wait_ge(S["dtraw_r"], gr + 1)
                a.activation(dtr[0:2 * RANK, gr, :], bank[gr][0:2 * RANK, :], ACT.Copy).then_inc(S["dtr_r"], 1)
                act.wait_ge(S["bc_r"], gr + 1)
                a.activation(BC[:, gr, :], bank[4 + gr][:], ACT.Copy).then_inc(S["bch_r"], 1)
            for gr in range(GROUPS):
                for c in range(gr * FRONT_W // GROUPS, (gr + 1) * FRONT_W // GROUPS):
                    round_weights(c)
                act.wait_ge(S["dtp_r"], gr + 1)
                act.wait_ge(S["sele_r"], 1)
                a.activation(dt[:, gr, :], bank[gr][:], ACT.Abs, bias=zero).then_inc(S["abs_r"], 1)
                act.wait_ge(S["abs_r"], gr + 1)
                a.activation(dt[:, gr, :], dt[:, gr, :], ACT.Sigmoid, scale=-1.0, bias=mln2).then_inc(S["lz_r"], 1)
                act.wait_ge(S["lz_r"], gr + 1)
                a.activation(lw[:, gr, :], dt[:, gr, :], ACT.Square, bias=zero).then_inc(S["lw_r"], 1)
            a.preload_act_table_set("natural_log_exp_and_others")

            def copy_b(k):
                act.wait_ge(S["pB"], k + 1)
                if k >= 2:
                    act.wait_ge(S["u_r"], k - 1)
                a.activation(Bs[:, k % 2], bank[B_BANK][:], ACT.Copy).then_inc(S["Bs_r"], 1)

            def decay(k):
                if k >= 2:
                    act.wait_ge(S["scan_r"], 2 * (k - 1))
                s = k % NS
                a.activation(bank[DECAY[k % 2]][:], dt[:, k // NS, :], ACT.Exp, scale=A[:, s:s + 1], bias=zero)\
                    .then_inc(S["dA_r"], 1)

            def scan_step(k):
                if k + 3 < STEPS:
                    copy_b(k + 3)
                if k + 2 < STEPS:
                    decay(k + 2)

            act.wait_ge(S["A_r"], 2)
            act.wait_ge(S["dt_r"], GROUPS)
            for k in range(3):
                copy_b(k)
            for k in range(2):
                decay(k)
            for k in range(SCAN0, SCAN1):
                scan_step(k)
                if k % 2 and FRONT_W + k // 2 < CHUNKS_W:
                    round_weights(FRONT_W + k // 2)

            def back(hb, i):
                bk = BACK[hb]
                if i == 2:
                    square(hb, HALVES + 2 * hb)
                if i in (3, 6):
                    a.preload_act_table_set("natural_log_exp_and_others")
                if i == 3:
                    inverse_std(hb, HALVES + 2 * hb, bk[2], eps)
                if i == 5:
                    square(hb, HALVES + 2 * hb + 1)
                if i == 6:
                    inverse_std(hb, HALVES + 2 * hb + 1, bk[2], eps)
                    act.wait_ge(S["tn_r"], hb + 1)
                    a.activation(tn_hi[:, hb, :], tn[:, hb, :], ACT.Copy).then_inc(S["tnh_r"], 1)
                if i == 7:
                    act.wait_ge(S["dif_r"], hb + 1)
                    a.activation(e1[:], e1[:], ACT.Exp, bias=zero).then_inc(S["ex_r"], 1)
                if i == 8:
                    act.wait_ge(S["tr_r"], BLK * (hb + 1))
                    a.activation(CE[:, hb, :], bank[bk[1]][0:64, :], ACT.Copy).then_inc(S["ceh_r"], 1)

            def round_scaled(k):
                act.wait_ge(S["xs_r"], k + 1)
                if k >= 2:
                    act.wait_ge(S["up_r"], FH * (k - 1))
                a.activation(xs_hi[:, k % 2, :], xs, ACT.Copy).then_inc(S["xsh_r"], 1)

            def gate_tanh(k, f):
                act.wait_ge(S["g_r"], FH * k + f + 1)
                if k:
                    act.wait_ge(S["hid_r"], FH * (k - 1) + f + 1)
                a.activation(th[:, f, :], bank[gate_bank(k, f)][:], ACT.Tanh, scale=0.5, bias=zero).then_inc(S["th_r"], 1)

            for k in range(SCAN1, POOL0):
                scan_step(k)
                if k % 2:
                    back(0, (k - SCAN1) // 2)
            back(0, PIECES - 1)
            a.preload_act_table_set("exp_and_others")
            round_scaled(0)
            for k in range(HALVES * E):
                for f in range(FH):
                    gate_tanh(k, f)
                    j = beside(FH * k + f)
                    if j is not None and j < STEPS:
                        scan_step(j)
                    if f == 0 and k + 1 < HALVES * E and k != E - 1:
                        round_scaled(k + 1)
                if k < E:
                    for i in back_pieces(k):
                        back(1, i)
                if k == E - 1:
                    round_scaled(E)

        @block.vector
        def _(dve):
            v = nc.vector

            def centre(hb, n, b, src):
                dve.wait_ge(S["mean_r"], n + 1)
                v.tensor_tensor(xm[:, hb, :], src, bank[b][:], ALU.subtract).then_inc(S["cen_r"], 1)

            def scale(hb, n, name="norm_r"):
                dve.wait_ge(S["rstd_r"], n + 1)
                v.tensor_tensor(xm[:, hb, :], xm[:, hb, :], sq[:, hb, :], ALU.mult).then_inc(S[name], 1)

            for hb in range(HALVES):
                centre(hb, hb, hb, X[:, hb, :])
            dve.wait_ge(S["sel1"], 4)
            v.tensor_copy(sel[:].rearrange("p s m -> p (s m)"), sel_tmp).then_inc(S["sel_r"], 1)
            dve.wait_ge(S["A_r"], 1)
            v.tensor_scalar(A[:], A[:], -1.0, None, ALU.mult).then_inc(S["A_r"], 1)
            for hb in range(HALVES):
                scale(hb, hb)
            dve.wait_ge(S["par_in"], 16)
            for hb in range(HALVES):
                dve.wait_ge(S["norm_r"], hb + 1)
                v.tensor_scalar(chk[:, hb, :], xm[:, hb, :], p("norm_g"), p("norm_b"), ALU.mult, ALU.add)\
                    .then_inc(S["chk_r"], 1)
            dve.wait_ge(S["sel_r"], 1)
            cw = COLS["conv_w"][0]
            for tap in range(TAPS):
                for gr in range(GROUPS):
                    w = par[:, cw + TAPS - 1 - tap:cw + TAPS - tap]
                    src = bank[4 + gr][:].rearrange("p (b t) -> p b t", t=T)[:, :, 0:T - tap]
                    dst = y[:, gr, :].rearrange("p (b t) -> p b t", t=T)[:, :, tap:T]
                    if tap == 0:
                        dve.wait_ge(S["xi_r"], gr + 1)
                        v.tensor_scalar(dst, src, w, None, ALU.mult).then_inc(S["conv_r"], 1)
                    else:
                        dve.wait_ge(S["conv_r"], (tap - 1) * GROUPS + gr + 1)
                        v.scalar_tensor_tensor(dst, src, w, dst, ALU.mult, ALU.add).then_inc(S["conv_r"], 1)
            dve.wait_ge(S["sel1"], 6)
            v.tensor_copy(sel_e[:].rearrange("p e m -> p (e m)"), sel_e_tmp).then_inc(S["sele_r"], 1)
            for gr in range(GROUPS):
                dve.wait_ge(S["bch_r"], gr + 1)
                for r in (slice(32, 64), slice(96, 128)):
                    v.tensor_tensor(BC[r, gr, :], bank[4 + gr][r, :], BC[r, gr, :].bitcast(F32), ALU.subtract)\
                        .then_inc(S["bcl_r"], 1)
            for gr in range(GROUPS):
                dve.wait_ge(S["lw_r"], gr + 1)
                v.tensor_scalar(lr[:, gr, :], lw[:, gr, :], LOG1P[4], LOG1P[3], ALU.mult, ALU.add).then_inc(S["lq_r"], 1)
            for i in (None, 2, 1):
                for gr in range(GROUPS):
                    dve.wait_ge(S["lq_r"], (0 if i is None else 3 - i) * GROUPS + gr + 1)
                    v.scalar_tensor_tensor(lr[:, gr, :], lr[:, gr, :], 0.0 if i is None else LOG1P[i], lw[:, gr, :],
                                           ALU.add, ALU.mult).then_inc(S["lq_r"], 1)
            for gr in range(GROUPS):
                dve.wait_ge(S["lq_r"], 3 * GROUPS + gr + 1)
                v.scalar_tensor_tensor(lr[:, gr, :], lr[:, gr, :], LOG1P[0], dt[:, gr, :], ALU.add, ALU.mult)\
                    .then_inc(S["lp_r"], 1)
            for gr in range(GROUPS):
                dve.wait_ge(S["lp_r"], gr + 1)
                v.scalar_tensor_tensor(dt[:, gr, :], bank[gr][:], 0.0, lr[:, gr, :], ALU.max, ALU.add)\
                    .then_inc(S["dt_r"], 1)

            def scan(k):
                dve.wait_ge(S["dA_r"], k + 1)
                dve.wait_ge(S["u_r"], k + 1)
                if k >= 2:
                    dve.wait_ge(S["hc_r"], k - 1)
                for b in range(2):
                    t = slice(b * T, (b + 1) * T)
                    v.tensor_tensor_scan(h[:, k % 2, t], bank[DECAY[k % 2]][:, t], u[:, k % 3, t], 0.0,
                                         ALU.mult, ALU.add).then_inc(S["scan_r"], 1)

            def weigh(k):
                dve.wait_ge(S["pC"], k + 1)
                dve.wait_ge(S["scan_r"], 2 * (k + 1))
                if k >= 3:
                    dve.wait_ge(S["red_r"], min(k - 2, POOL0))
                if k - 3 > POOL0:
                    dve.wait_ge(S["acc_r"], acc_count(k - 2))
                dst = y[:, k // NS, :] if k == POOL0 else hc[:, k % 3]
                v.tensor_tensor(dst, h[:, k % 2], bank[c_bank(k)][:], ALU.mult).then_inc(S["hc_r"], 1)

            def finish_group(gr):
                if gr < GROUPS - 1:
                    dve.wait_ge(S["red_r"], NS * (gr + 1))
                    total = bank[STATE_SUM[gr]][:]
                else:
                    dve.wait_ge(S["acc_r"], acc_count(STEPS))
                    total = y[:, gr, :]
                v.scalar_tensor_tensor(y[:, gr, :], xc[:, gr, :], p("D"), total, ALU.mult, ALU.add)\
                    .then_inc(S["yg_r"], 1)
                dve.wait_ge(S["yg_r"], gr + 1)
                v.tensor_tensor(y[:, gr, :], y[:, gr, :], zs[:, gr, :], ALU.mult).then_inc(S["y_r"], 1)

            def back(hb, i):
                bk = BACK[hb]
                if i == 0:
                    finish_group(PAIRS * hb + 1)
                if i == 1:
                    dve.wait_ge(S["op_r"], hb + 1)
                    v.scalar_tensor_tensor(chk[:, hb, :], chk[:, hb, :], p("skip"), bank[bk[0]][:], ALU.mult, ALU.add)\
                        .then_inc(S["y2_r"], 1)
                if i == 2:
                    centre(hb, HALVES + 2 * hb, bk[1], chk[:, hb, :])
                if i == 3:
                    scale(hb, HALVES + 2 * hb)
                    dve.wait_ge(S["norm_r"], HALVES + hb + 1)
                    v.tensor_scalar(chk[:, hb, :], xm[:, hb, :], p("norm_g"), p("norm_b"), ALU.mult, ALU.add)\
                        .then_inc(S["y3_r"], 1)
                if i == 4:
                    dve.wait_ge(S["pj_r"], hb + 1)
                    v.scalar_tensor_tensor(X[:, hb, :], bank[bk[0]][:], p("proj_b"), X[:, hb, :], ALU.add, ALU.add)\
                        .then_inc(S["x1_r"], 1)
                if i == 5:
                    centre(hb, HALVES + 2 * hb + 1, bk[1], X[:, hb, :])
                if i == 6:
                    scale(hb, HALVES + 2 * hb + 1, "tn_r")
                    dve.wait_ge(S["tnh_r"], hb + 1)
                    v.tensor_tensor(tn_lo[:, hb, :], tn[:, hb, :], tn_hi[:, hb, :].bitcast(F32), ALU.subtract)\
                        .then_inc(S["tnl_r"], 1)
                if i == 7:
                    dve.wait_ge(S["lg_r"], hb + 1)
                    v.tensor_copy(L[:].rearrange("p b e -> p (b e)"), bank[bk[0]][:, 0:BLK * E]).then_inc(S["L_r"], 1)
                    dve.wait_ge(S["L_r"], hb + 1)
                    for b in range(BLK):
                        v.max(top[:, b, :], L[:, b, :]).then_inc(S["top_r"], 1)
                    for b in range(BLK):
                        dve.wait_ge(S["top_r"], BLK * hb + b + 1)
                        v.max_index(topi[:, b, :], top[:, b, :], L[:, b, :]).then_inc(S["topi_r"], 1)
                    v.tensor_tensor(e1[:], top[:, :, 1:2], top[:, :, 0:1], ALU.subtract).then_inc(S["dif_r"], 1)
                    dve.wait_ge(S["topi_r"], BLK * (hb + 1))
                    v.tensor_copy(topf[:], topi[:, :, 0:2]).then_inc(S["topf_r"], 1)
                if i == 8:
                    dve.wait_ge(S["topf_r"], hb + 1)
                    for j in range(2):
                        v.tensor_tensor(oh[:, j], iota_e[:], topf[:, :, j:j + 1].broadcast_to([P, BLK, E]),
                                        ALU.is_equal).then_inc(S["eq_r"], 1)
                    dve.wait_ge(S["ex_r"], hb + 1)
                    v.tensor_scalar(w01[:, :, 0:1], e1[:], 1.0, None, ALU.add).then_inc(S["sum_r"], 1)
                    dve.wait_ge(S["sum_r"], hb + 1)
                    v.reciprocal(w01[:, :, 0:1], w01[:, :, 0:1]).then_inc(S["w0_r"], 1)
                    dve.wait_ge(S["w0_r"], hb + 1)
                    v.tensor_tensor(w01[:, :, 1:2], e1[:], w01[:, :, 0:1], ALU.mult).then_inc(S["w1_r"], 1)
                    dve.wait_ge(S["w1_r"], hb + 1)
                    for j in range(2):
                        dve.wait_ge(S["eq_r"], 2 * hb + j + 1)
                        v.tensor_tensor(oh[:, j], oh[:, j], w01[:, :, j:j + 1].broadcast_to([P, BLK, E]), ALU.mult)\
                            .then_inc(S["ow_r"], 1)
                    dve.wait_ge(S["ow_r"], 2 * hb + 2)
                    for part in range(2):
                        v.tensor_tensor(cpad[:, :, 32 * part:32 * part + E], oh[:, 0], oh[:, 1], ALU.add)\
                            .then_inc(S["ce_r"], 1)
                    dve.wait_ge(S["ceh_r"], hb + 1)
                    v.tensor_tensor(CE[32:64, hb, :], bank[bk[1]][32:64, :], CE[32:64, hb, :].bitcast(F32),
                                    ALU.subtract).then_inc(S["cel_r"], 1)

            def scale_tokens(k):
                dve.wait_ge(S["ceb_r"], k + 1)
                if k:
                    dve.wait_ge(S["xsl_r"], k)
                v.tensor_tensor(xs, tn[:, k // E, :], bank[SPREAD][:], ALU.mult).then_inc(S["xs_r"], 1)

            def gate(k, f):
                dve.wait_ge(S["th_r"], FH * k + f + 1)
                v.scalar_tensor_tensor(th[:, f, :], th[:, f, :], 1.0, bank[gate_bank(k, f)][:], ALU.add, ALU.mult)\
                    .then_inc(S["m_r"], 1)

            def hidden(k, f):
                dve.wait_ge(S["up_r"], FH * k + f + 1)
                dve.wait_ge(S["m_r"], FH * k + f + 1)
                if k >= 2:
                    dve.wait_ge(S["yd_r"], FH * (k - 2) + f + 1)
                v.tensor_tensor(hid[k % 2][:, f, :], th[:, f, :], bank[up_bank(k, f)][:], ALU.mult).then_inc(S["hid_r"], 1)

            for k in range(SCAN0, SCAN1):
                scan(k)
                if k:
                    weigh(k - 1)
                if k == NS + 3:
                    finish_group(0)
            for k in range(SCAN1, POOL0):
                scan(k)
                weigh(k - 1)
                if k % 2:
                    back(0, (k - SCAN1) // 2)
            weigh(POOL0 - 1)
            back(0, PIECES - 1)
            finish_group(2)
            scale_tokens(0)
            for k in range(HALVES * E):
                for f in range(FH):
                    gate(k, f)
                    j = beside(FH * k + f)
                    if j is not None and j < STEPS:
                        scan(j)
                    hidden(k, f)
                    if j is not None and j > POOL0:
                        weigh(j - 1)
                    if f == 0 and k + 1 < HALVES * E and k != E - 1:
                        scale_tokens(k + 1)
                if k < E:
                    for i in back_pieces(k):
                        back(1, i)
                if k % E == E - 1:
                    if k == E - 1:
                        scale_tokens(E)
                    hb = k // E
                    dve.wait_ge(S["yd_r"], (k + 1) * FH)
                    v.tensor_tensor(X[:, hb, :], X[:, hb, :], bank[YSUM][:], ALU.add).then_inc(S["res_r"], 1)

        @block.tensor
        def _(pe):
            t = nc.tensor
            pe.wait_ge(S["const0"], 2)

            def mm(o, w, r, name, start=True, stop=True):
                return t.matmul(o, w, r, start=start, stop=stop).then_inc(S[name], 1)

            def mean(b, src):
                mm(bank[b][:], mean_w[:], src, "mean_r")

            def variance(hb, n, b, w):
                pe.wait_ge(S["sq_r"], n + 1)
                mm(bank[b][:], w[:], sq[:, hb, :], "var_r")

            for hb in range(HALVES):
                pe.wait_ge(S[f"x_in{hb}"], 16)
                mean(hb, X[:, hb, :])
            for hb in range(HALVES):
                variance(hb, hb, 2 + hb, var_in_w)
            pe.wait_ge(S["par_in"], 16)
            for hb in range(HALVES):
                pe.wait_ge(S["chk_r"], hb + 1)
                for q in range(PAIRS):
                    rows = slice(64 * q, 64 * q + 64)
                    mm(bank[4 + 2 * hb + q][:], p("in_x")[rows], chk[rows, hb, :], "xi_r")
            pe.wait_ge(S["cen_r"], HALVES)
            pe.wait_ge(S["ln_r"], HALVES)
            for hb in range(HALVES):
                for q in range(PAIRS):
                    rows = slice(64 * q, 64 * q + 64)
                    mm(bank[2 * hb + q][:], p("in_z")[rows], chk[rows, hb, :], "z_r")
            for gr in range(GROUPS):
                pe.wait_ge(S["xc_r"], gr + 1)
                pe.wait_ge(S["zs_r"], gr + 1)
                mm(bank[gr][0:2 * RANK, :], p("dt_in"), xc[:, gr, :], "dtraw_r")
                mm(bank[4 + gr][:], p("bc"), xc[:, gr, :], "bc_r")
            for gr in range(GROUPS):
                pe.wait_ge(S["dtr_r"], gr + 1)
                mm(bank[gr][:], p("dt_out")[0:DTK], dtr[:, gr, :], "dtp_r")
            pe.wait_ge(S["sel_r"], 1)
            pe.wait_ge(S["ident_r"], 1)
            pe.wait_ge(S["bcl_r"], 2 * GROUPS)
            pe.wait_ge(S["dt_r"], GROUPS)

            def sum_state(k):
                gr, s = divmod(k, NS)
                if k == 2 * NS:
                    pe.wait_ge(S["yg_r"], 2)
                elif s == 0 and gr:
                    pe.wait_ge(S["hc_r"], k)
                pe.wait_ge(S["hc_r"], k + 1)
                mm(bank[STATE_SUM[gr]][:], ident[:], hc[:, k % 3], "red_r", s == 0, s == NS - 1)

            def spread_b(k):
                if k:
                    pe.wait_ge(S["Bs_r"], k)
                mm(bank[B_BANK][:], sel[0:64, k % NS, :], BC[0:64, k // NS, :], "pB")

            def spread_c(k):
                if c_before(k):
                    pe.wait_ge(S["hc_r"], c_before(k))
                mm(bank[c_bank(k)][:], sel[64:128, k % NS, :], BC[64:128, k // NS, :], "pC")

            for k in range(3):
                spread_b(k)
            for k in range(2):
                spread_c(k)
            for k in range(SCAN0, SCAN1):
                spread_b(k + 3)
                if k + 2 < SCAN1:
                    spread_c(k + 2)
                if k >= 2:
                    sum_state(k - 2)

            def back(hb, i):
                bk = BACK[hb]
                if i == 1:
                    for q in range(PAIRS):
                        pe.wait_ge(S["y_r"], 2 * hb + q + 1)
                        o = t.matmul(bank[bk[0]][64 * q:64 * q + 64, :], p("out"), y[:, 2 * hb + q, :],
                                     start=True, stop=True)
                    o.then_inc(S["op_r"], 1)
                if i == 2:
                    pe.wait_ge(S["y2_r"], hb + 1)
                    mean(bk[1], chk[:, hb, :])
                if i == 3:
                    variance(hb, HALVES + 2 * hb, bk[2], mean_w)
                if i == 4:
                    pe.wait_ge(S["y3_r"], hb + 1)
                    mm(bank[bk[0]][:], p("proj"), chk[:, hb, :], "pj_r")
                if i == 5:
                    pe.wait_ge(S["x1_r"], hb + 1)
                    mean(bk[1], X[:, hb, :])
                if i == 6:
                    variance(hb, HALVES + 2 * hb + 1, bk[2], mean_w)
                if i == 7:
                    pe.wait_ge(S["tn_r"], hb + 1)
                    for b in range(BLK):
                        o = t.matmul(bank[bk[0]][:, b * E:(b + 1) * E], tn[:, hb, b * P:(b + 1) * P], p("router"),
                                     start=True, stop=True)
                    o.then_inc(S["lg_r"], 1)
                if i == 8:
                    pe.wait_ge(S["ce_r"], 2 * (hb + 1))
                    for b in range(BLK):
                        t.transpose(bank[bk[1]][0:64, b * P:(b + 1) * P], cpad[:, b, :], ident[:])\
                            .then_inc(S["tr_r"], 1)

            def spread_gate(k):
                pe.wait_ge(S["cel_r"], k // E + 1)
                if k:
                    pe.wait_ge(S["xs_r"], k)
                mm(bank[SPREAD][:], sel_e[:, k % E, :], CE[:, k // E, :], "ceb_r")

            def product(b, w, k, f, hi, lo, name):
                ws = slice(f * P, (f + 1) * P)
                t.matmul(bank[b][:], W_hi[w][:, k % E, ws], hi, start=True, stop=False)
                t.matmul(bank[b][:], W_hi[w][:, k % E, ws], lo, start=False, stop=False)
                mm(bank[b][:], W_lo[w][:, k % E, ws], hi, name, False, True)

            def down(k, f):
                pe.wait_ge(S["hid_r"], FH * k + f + 1)
                e = k % E
                if e == 0 and f == 0 and k:
                    pe.wait_ge(S["res_r"], k // E)
                mm(bank[YSUM][:], Wd[:, e, f, :], hid[k % 2][:, f, :], "yd_r",
                   e == 0 and f == 0, e == E - 1 and f == FH - 1)

            for k in range(SCAN1, POOL0):
                spread_b(k + 3)
                sum_state(k - 2)
                spread_c(k)
                if k % 2:
                    back(0, (k - SCAN1) // 2)
            sum_state(POOL0 - 2)
            sum_state(POOL0 - 1)
            back(0, PIECES - 1)
            pe.wait_ge(S["sele_r"], 1)
            pe.wait_ge(S["wd_in"], 16)
            pe.wait_ge(S["w_lo"], CHUNKS_W)
            pe.wait_ge(S["yg_r"], 3)
            spread_gate(0)
            for k in range(HALVES * E):
                hb = k // E
                if k == E:
                    pe.wait_ge(S["cel_r"], HALVES)
                for f in range(FH):
                    slot = FH * k + f
                    if f == 0:
                        pe.wait_ge(S["tnl_r"], hb + 1)
                    if slot:
                        pe.wait_ge(S["m_r"], slot if gate_bank(k, f) == gate_bank((slot - 1) // FH, 1 - f) else slot - 1)
                    product(gate_bank(k, f), 0, k, f, tn_hi[:, hb, :], tn_lo[:, hb, :], "g_r")
                    j = beside(slot)
                    if j is not None:
                        if j + 3 < STEPS:
                            spread_b(j + 3)
                        if j > POOL0:
                            spread_c(j - 1)
                    if f == 0:
                        pe.wait_ge(S["xsl_r"], k + 1)
                    if slot:
                        pe.wait_ge(S["hid_r"], slot if up_bank(k, f) == up_bank((slot - 1) // FH, 1 - f) else slot - 1)
                    product(up_bank(k, f), 1, k, f, xs_hi[:, k % 2, :], xs_lo[:, k % 2, :], "up_r")
                    if f == 0 and k + 1 < HALVES * E and k != E - 1:
                        spread_gate(k + 1)
                    if k % E:
                        down(k - 1, f)
                if k < E:
                    for i in back_pieces(k):
                        back(1, i)
                if k % E == E - 1:
                    if k == E - 1:
                        spread_gate(E)
                    for f in range(FH):
                        down(k, f)


def kernel(**inputs):
    import concourse.bacc as bacc
    from concourse.bass_utils import run_bass_kernel_spmd as run

    a = {k.removeprefix("L0_"): np.asarray(v) for k, v in inputs.items()}
    par = np.zeros((P, NPACK), np.float32)

    def put(name, m, row=0, col=0):
        c0 = COLS[name][0] + col
        par[row:row + m.shape[0], c0:c0 + m.shape[1]] = m

    put("norm_g", a["conv_norm_g"][:, None])
    put("norm_b", a["conv_norm_b"][:, None])
    put("proj_b", a["conv_proj_b"][:, None])
    put("skip", np.broadcast_to(a["conv_skip_scale"][:, None], (P, 1)))
    put("proj", a["conv_proj_w"].T)
    put("router", a["ffn_router_w"].T)
    for j in range(2):
        for name, key in (("conv_b", "conv_conv_b"), ("D", "conv_D_param")):
            put(name, a[key][:, None], DI * j)
        put("conv_w", a["conv_conv_w"], DI * j)
        put("A_log", a["conv_A_log"], DI * j)
        put("dt_in", a["conv_x_proj_w"].T[:, 0:RANK], DI * j, RANK * j)
        put("dt_out", a["conv_dt_proj_w"].T, RANK * j, DI * j)
        put("dt_out", a["conv_dt_proj_b"][None, :], 2 * RANK, DI * j)
        put("out", a["conv_out_proj_w"].T, DI * j, DM * j)
        for part in range(2):
            for i in range(2):
                put("bc", a["conv_x_proj_w"].T[:, RANK + NS * i:RANK + NS * (i + 1)], DI * j, 64 * i + 32 * part + NS * j)
    for q in range(CHUNKS):
        put("in_x", a["conv_in_proj_w"].T[:, 0:DI], DM * q, DI * (q % 2))
        put("in_z", a["conv_in_proj_w"].T[:, DI:2 * DI], DM * q, DI * (q % 2))
    arrays = {"x": np.ascontiguousarray(a["x"].reshape(BATCH, C, T)), "params": par, "gate_w": a["ffn_gate_w"],
              "up_w": a["ffn_up_w"], "down_w": a["ffn_down_w"]}

    nc = bacc.Bacc("TRN2", target_bir_lowering=False, num_devices=1)
    args = [nc.dram_tensor(k, v.shape, F32, kind="ExternalInput").ap() for k, v in arrays.items()]
    out = nc.dram_tensor("out", (BATCH, C, T), F32, kind="ExternalOutput").ap()
    build(nc, *args, out)
    r = run(nc, [arrays], core_ids=[0])
    return r.results[0]["out"].reshape(BATCH, C, 16, 16)
```

```python
from contextlib import ExitStack

import numpy as np
import concourse.bass as bass
from concourse import mybir

P = 128
BATCH, C, T = 4, 128, 256
CHUNKS, DM, DI = 4, 32, 64
PAIRS = CHUNKS // 2
NS = 16
RANK = 2
TAPS = 4
E, F = 16, 256
FH = F // P
HALVES = 2
N = BATCH * T // HALVES
GROUPS = HALVES * PAIRS
DTK = 2 * RANK + 1
LN2 = float(np.log(2.0))
LOG1P = (2.00000001, 0.66666317, 0.40024839, 0.27961494, 0.28174741)
BLK = N // P
EPS_IN, EPS = 1e-6, 1e-5
WCH = 2
CHUNKS_W = 2 * E // WCH
SCAN0, SCAN1 = 0, PAIRS * NS
STEPS = GROUPS * NS
POOL0 = 3 * NS
LEAD_END = POOL0 + 2
SCAN_SLOTS = 16
STAGES = 6
ACT_ROUNDS = 6
BACK_STEP = SCAN1 + 1
WARM_STEPS = 8
ITEMS = 13

F32, F32R, U32 = mybir.dt.float32, mybir.dt.float32r, mybir.dt.uint32
ALU, ACT = mybir.AluOpType, mybir.ActivationFunctionType

COLS = {}
_at = 0
for _name, _width in (("norm_g", 1), ("norm_b", 1), ("proj_b", 1), ("skip", 1), ("conv_w", TAPS), ("conv_b", 1),
                      ("D", 1), ("A_log", NS), ("in_x", P), ("in_z", P), ("bc", P), ("dt_in", 2 * RANK),
                      ("dt_out", P), ("out", 2 * DM), ("proj", P), ("router", E)):
    COLS[_name] = (_at, _at + _width)
    _at += _width
NPACK = _at


def build(nc, x, params, gate_w, up_w, down_w, out):
    with ExitStack() as ctx:
        def sb(name, shape, dt=F32):
            return ctx.enter_context(nc.sbuf_tensor(name, shape, dt))

        bank = [ctx.enter_context(nc.psum_tensor(f"bank{i}", [P, N], F32)) for i in range(8)]
        STATE_SUM = (7, 6, 7)
        BACK = ((4, 5), (2, 3))
        YSUM, SPREAD = 6, 7
        GATE, UP = (4, 0), (5, 1)

        def b_bank(k):
            return (2, 1)[k % 2] if k < LEAD_END else 2

        def c_bank(k):
            return (3, 0)[k % 2] if k < LEAD_END else 3

        def dt_bank(gr):
            return 3 + gr if gr else 0

        def before(bank_of, k):
            return max((j + 1 for j in range(k) if bank_of(j) == bank_of(k)), default=0)

        X = sb("X", [P, HALVES, N])
        par = sb("par", [P, NPACK])
        W_hi = [sb("Wg_hi", [P, E, F], F32R), sb("Wu_hi", [P, E, F], F32R)]
        W_lo = [sb("Wg_lo", [P, E, F], F32R), sb("Wu_lo", [P, E, F], F32R)]
        Wd = sb("Wd", [P, E, FH, C])
        mean_w = sb("mean_w", [P, P])
        var_in_w = sb("var_in_w", [P, P])
        cst = sb("cst", [P, 5])
        ident = sb("ident", [P, P])
        iota_e = sb("iota_e", [P, BLK, E])
        sel = sb("sel", [P, NS, P], F32R)
        sel_e = sb("sel_e", [P // 2, E], F32R)
        unit = sb("unit", [P, 32])
        A = sb("A", [P, NS])
        xm = sb("xm", [P, HALVES, N])
        sq = sb("sq", [P, HALVES, N])
        chk = sb("chk", [P, HALVES, N])
        xc = sb("xc", [P, GROUPS, N])
        zs = sb("zs", [P, GROUPS, N])
        dt = sb("dt", [P, GROUPS, N])
        dtx = sb("dtx", [P, GROUPS, N])
        BC = sb("BC", [P, GROUPS, N], F32R)
        y = sb("y", [P, GROUPS, N])
        ring = sb("ring", [P, 3 + 3 + 2 + 3 + 3, N])
        u, Bs, h, hc, dA = ring[:, 0:3], ring[:, 3:6], ring[:, 6:8], ring[:, 8:11], ring[:, 11:14]
        L = sb("L", [P, BLK, E])
        top = sb("top", [P, BLK, 8])
        topi = sb("topi", [P, BLK, 8], U32)
        topf = sb("topf", [P, BLK, 2])
        w01 = sb("w01", [P, BLK, 2])
        e1 = sb("e1", [P, BLK, 1])
        oh = sb("oh", [P, 2, BLK, E])
        cpad = sb("cpad", [P, BLK, P // 2])
        CE = sb("CE", [P // 2, HALVES, N], F32R)
        tn_hi = sb("tn_hi", [P, HALVES, N], F32R)
        tn_lo = sb("tn_lo", [P, HALVES, N], F32R)
        xs_hi = sb("xs_hi", [P, 2, N], F32R)
        xs_lo = sb("xs_lo", [P, 2, N], F32R)
        xs = xc[:, 0, :]
        th = dt[:, 0:FH]
        hid = (y[:, 0:FH], zs[:, 0:FH])
        tn = xm
        dtr = ring[0:DTK, 5:5 + GROUPS]
        lr = y
        lw = dtx
        stages = [ring[:, 9 + i] for i in range(4)] + [sq[:, hb] for hb in range(HALVES)]

        def stage(c):
            return stages[c % STAGES].rearrange("p (e f) -> p e f", f=F)

        eps_in, eps, zero, mln2, rest_row = (cst[:, i:i + 1] for i in range(5))

        def p(name):
            a, b = COLS[name]
            return par[:, a:b]

        names = ("x_in0 x_in1 par_in wd_in const0 const1 ident_r sel0 sel1 sel_r sele_r A_r cen_r sq_r mean_r var_r ln_r "
                 "rstd_r norm_r chk_r xi_r z_r conv_r xc_r zs_r bc_r dtraw_r dtr_r dtp_r bch_r bcl_r abs_r lz_r lw_r "
                 "lq_r lp_r dt_r dtx_r pB pC Bs_r dA_r u_r scan_r hc_r red_r acc_r yg_r y_r op_r y2_r y3_r "
                 "pj_r x1_r tn_r tnh_r tnl_r lg_r L_r top_r topi_r topf_r dif_r ex_r sum_r w0_r w1_r eq_r ow_r ce_r "
                 "tr_r ceh_r cel_r ceb_r xs_r xsh_r xsl_r g_r up_r th_r m_r hid_r yd_r res_r out_d "
                 "w_hi w_hi2 w_lo rest0").split() + [f"w_in{c}" for c in range(CHUNKS_W)]
        S = {n: ctx.enter_context(nc.semaphore(n)) for n in names}

        def acc_count(k):
            return sum(1 for i in range(POOL0, k) if i % NS)

        step_at = {t * SCAN_SLOTS // (STEPS - LEAD_END): LEAD_END + t for t in range(STEPS - LEAD_END)}
        step_at[SCAN_SLOTS] = STEPS

        def beside(slot):
            return step_at.get(slot)

        def back_item(slot):
            i = slot - SCAN_SLOTS - 1
            return i if i in range(ITEMS) and slot < FH * E else None

        block = ctx.enter_context(nc.Block())

        @block.sync
        def _(sp):
            for hb in range(HALVES):
                sp.dma_start(X[:, hb, :].rearrange("p (b t) -> p b t", t=T),
                             x[2 * hb:2 * hb + 2].rearrange("b c t -> c b t")).then_inc(S[f"x_in{hb}"], 16)
            for c in range(CHUNKS_W):
                if c >= STAGES:
                    sp.wait_ge(S["w_lo"], c - STAGES + 1)
                elif c >= STAGES - HALVES:
                    sp.wait_ge(S["norm_r"], c - (STAGES - HALVES) + 1)
                src = (gate_w, up_w)[c * WCH // E][c * WCH % E:c * WCH % E + WCH]
                sp.dma_start(stage(c), src.rearrange("e h f -> h e f"))\
                    .then_inc(S[f"w_in{c}"], 16)
                if c == 5:
                    sp.dma_start(Wd[:], down_w.rearrange("e (f p) h -> p e f h", p=P)).then_inc(S["wd_in"], 16)
            for hb in range(HALVES):
                sp.wait_ge(S["res_r"], hb + 1)
                sp.dma_start(out[2 * hb:2 * hb + 2].rearrange("b c t -> c b t"),
                             X[:, hb, :].rearrange("p (b t) -> p b t", t=T)).then_inc(S["out_d"], 16)
            sp.wait_ge(S["out_d"], 16 * HALVES)

        @block.gpsimd
        def _(pool):
            g = nc.gpsimd
            g.memset(mean_w[:], 1.0 / C).then_inc(S["const0"], 1)
            g.memset(var_in_w[:], (1.0 + EPS) / C).then_inc(S["const0"], 1)
            for i, value in enumerate((EPS_IN * EPS, EPS, 0.0, -LN2)):
                g.memset(cst[:, i:i + 1], value).then_inc(S["const0"], 1)
            g.memset(rest_row, 0.0).then_inc(S["rest0"], 1)
            for row in (32, 96):
                pool.wait_ge(S["rest0"], 1 + row // 96)
                g.memset(cst[row:row + 32, 4:5], -1.0).then_inc(S["rest0"], 1)
            pool.wait_ge(S["rest0"], 3)
            g.memset(unit[:], 0.0).then_inc(S["sel0"], 1)
            pool.wait_ge(S["sel0"], 1)
            for q in range(4):
                v = unit[32 * q:32 * q + 32, :]
                g.affine_select(out=v, in_=v, compare_op=ALU.not_equal, fill=1.0, base=0,
                                pattern=[[-1, 32]], channel_multiplier=1).then_inc(S["sel1"], 1)
            pool.wait_ge(S["sel1"], 4)
            g.memset(dtr, 1.0).then_inc(S["const1"], 1)
            g.memset(cpad[:], 0.0).then_inc(S["const1"], 1)
            g.iota(iota_e[:], pattern=[[0, BLK], [1, E]], base=0, channel_multiplier=0,
                   allow_small_or_imprecise_dtypes=True).then_inc(S["const1"], 1)
            g.memset(ident[:], 0.0).then_inc(S["sel0"], 1)
            pool.wait_ge(S["sel0"], 2)
            g.affine_select(out=ident[:], in_=ident[:], compare_op=ALU.not_equal, fill=1.0, base=0,
                            pattern=[[-1, P]], channel_multiplier=1).then_inc(S["ident_r"], 1)
            def split_rest(c):
                if c < ACT_ROUNDS:
                    pool.wait_ge(S["w_hi"], c + 1)
                else:
                    pool.wait_ge(S["w_hi2"], c - ACT_ROUNDS + 1)
                w, es = c * WCH // E, slice(c * WCH % E, c * WCH % E + WCH)
                g.tensor_tensor(W_lo[w][:, es], stage(c),
                                W_hi[w][:, es].bitcast(F32), ALU.subtract).then_inc(S["w_lo"], 1)

            for c in range(CHUNKS_W - 4):
                split_rest(c)
            def scan_source(gr):
                pool.wait_ge(S["dt_r"], gr + 1)
                g.tensor_tensor(dtx[:, gr, :], dt[:, gr, :], xc[:, gr, :], ALU.mult).then_inc(S["dtx_r"], 1)

            def scan_input(k):
                pool.wait_ge(S["Bs_r"], k + 1)
                if k >= 3:
                    pool.wait_ge(S["scan_r"], 2 * (k - 2))
                g.tensor_tensor(u[:, k % 3], dtx[:, k // NS, :], Bs[:, k % 3], ALU.mult).then_inc(S["u_r"], 1)

            def add_state(k):
                if k > POOL0:
                    pool.wait_ge(S["hc_r"], k + 1)
                    pool.wait_ge(S["acc_r"], acc_count(k))
                    g.tensor_tensor(y[:, k // NS, :], y[:, k // NS, :], hc[:, k % 3], ALU.add).then_inc(S["acc_r"], 1)

            def split_scaled(k):
                pool.wait_ge(S["xsh_r"], k + 1)
                if k >= 2:
                    pool.wait_ge(S["up_r"], FH * (k - 1))
                g.tensor_tensor(xs_lo[:, k % 2, :], xs, xs_hi[:, k % 2, :].bitcast(F32), ALU.subtract)\
                    .then_inc(S["xsl_r"], 1)

            scan_source(0)
            for c in range(CHUNKS_W - 4, CHUNKS_W):
                split_rest(c)
            for k in range(SCAN0, LEAD_END + 1):
                if k % NS == 0:
                    pool.wait_ge(S["dtx_r"], k // NS + 1)
                scan_input(k)
                if k % 6 == 2 and k // 6 in range(1, GROUPS):
                    scan_source(k // 6)
                add_state(k - 2)
            split_scaled(0)
            for slot in range(FH * E):
                k = beside(slot)
                if k is not None and k + 1 < STEPS:
                    scan_input(k + 1)
                if slot % FH == 0 and slot // FH + 1 < E:
                    split_scaled(slot // FH + 1)
                if k is not None:
                    add_state(k - 1)
            for e in range(E):
                split_scaled(E + e)

        @block.scalar
        def _(act):
            a = nc.scalar
            act.dma_start(par[:], params).then_inc(S["par_in"], 16)
            a.preload_act_table_set("natural_log_exp_and_others")
            act.wait_ge(S["par_in"], 16)
            act.wait_ge(S["const0"], 6)
            a.activation(A[:], p("A_log"), ACT.Exp, bias=zero).then_inc(S["A_r"], 1)

            def square(hb, n):
                act.wait_ge(S["cen_r"], n + 1)
                a.activation(sq[:, hb, :], xm[:, hb, :], ACT.Square, bias=zero).then_inc(S["sq_r"], 1)

            def inverse_std(hb, n, b, bias):
                act.wait_ge(S["var_r"], n + 1)
                a.activation(sq[:, hb, :], bank[b][:], ACT.Ln, bias=bias).then_inc(S["ln_r"], 1)
                act.wait_ge(S["ln_r"], n + 1)
                a.activation(sq[:, hb, :], sq[:, hb, :], ACT.Exp, scale=-0.5, bias=zero).then_inc(S["rstd_r"], 1)

            def round_weights(c):
                act.wait_ge(S[f"w_in{c}"], 16)
                w, es = c * WCH // E, slice(c * WCH % E, c * WCH % E + WCH)
                a.activation(W_hi[w][:, es], stage(c), ACT.Copy)\
                    .then_inc(S["w_hi"], 1)

            for hb in range(HALVES):
                square(hb, hb)
            for hb in range(HALVES):
                inverse_std(hb, hb, 2 + hb, eps_in)
            a.preload_act_table_set("silu_and_others")
            def copy_rank(gr):
                act.wait_ge(S["dtraw_r"], gr + 1)
                a.activation(dtr[0:2 * RANK, gr, :], bank[gr][0:2 * RANK, :], ACT.Copy).then_inc(S["dtr_r"], 1)

            def round_bc(gr):
                act.wait_ge(S["bc_r"], gr + 1)
                a.activation(BC[:, gr, :], bank[4 + gr][:], ACT.Copy).then_inc(S["bch_r"], 1)

            def magnitude(gr):
                act.wait_ge(S["dtp_r"], gr + 1)
                a.activation(dt[:, gr, :], bank[dt_bank(gr)][:], ACT.Abs, bias=zero).then_inc(S["abs_r"], 1)

            def softplus_z(gr):
                act.wait_ge(S["abs_r"], gr + 1)
                a.activation(dt[:, gr, :], dt[:, gr, :], ACT.Sigmoid, scale=-1.0, bias=mln2).then_inc(S["lz_r"], 1)

            def gate_z(gr):
                act.wait_ge(S["z_r"], gr + 1)
                a.activation(zs[:, gr, :], bank[gr][:], ACT.Silu, bias=zero).then_inc(S["zs_r"], 1)

            def convolved(gr):
                hb, q = divmod(gr, PAIRS)
                act.wait_ge(S["conv_r"], TAPS * PAIRS * hb + (TAPS - 1) * PAIRS + q + 1)
                a.activation(xc[:, gr, :], y[:, gr, :], ACT.Silu, bias=p("conv_b")).then_inc(S["xc_r"], 1)

            for c in range(4):
                round_weights(c)
            for gr in (0, 1):
                gate_z(gr)
            for gr in (0, 1):
                convolved(gr)
            for gr in (2, 3):
                gate_z(gr)
            act.wait_ge(S["const1"], 3)
            for gr in (0, 1):
                copy_rank(gr)
                round_bc(gr)
            for c in range(4, ACT_ROUNDS):
                round_weights(c)
            for gr in (2, 3):
                convolved(gr)
            for gr in (0, 1):
                magnitude(gr)
            a.preload_act_table_set("sigmoid_and_others")
            softplus_z(0)
            softplus_z(1)
            for gr in (2, 3):
                copy_rank(gr)
                round_bc(gr)
            for gr in (2, 3):
                magnitude(gr)
            def copy_b(k):
                act.wait_ge(S["pB"], k + 1)
                if k >= 3:
                    act.wait_ge(S["u_r"], k - 2)
                a.activation(Bs[:, k % 3], bank[b_bank(k)][:], ACT.Copy).then_inc(S["Bs_r"], 1)

            def decay(k):
                if k >= 3:
                    act.wait_ge(S["scan_r"], 2 * (k - 2))
                s = k % NS
                a.activation(dA[:, k % 3], dt[:, k // NS, :], ACT.Exp, scale=A[:, s:s + 1], bias=zero)\
                    .then_inc(S["dA_r"], 1)

            def scan_step(k):
                if k + 3 < STEPS:
                    copy_b(k + 3)
                if k + 2 < STEPS:
                    decay(k + 2)

            for k in range(3):
                copy_b(k)
            for gr in (2, 3):
                softplus_z(gr)
            a.preload_act_table_set("natural_log_exp_and_others")
            act.wait_ge(S["A_r"], 2)
            act.wait_ge(S["w_lo"], CHUNKS_W)
            act.wait_ge(S["dt_r"], 1)
            for k in range(2):
                decay(k)
            for k in range(SCAN0, SCAN1):
                if (k + 2) % NS == 0:
                    act.wait_ge(S["dt_r"], (k + 2) // NS + 1)
                scan_step(k)

            def back(hb, i):
                bk = BACK[hb]
                if i == 3:
                    square(hb, HALVES + 2 * hb)
                if i in (4, 8) and hb:
                    a.preload_act_table_set("natural_log_exp_and_others")
                if i == 4:
                    inverse_std(hb, HALVES + 2 * hb, bk[0], eps)
                if i == 7:
                    square(hb, HALVES + 2 * hb + 1)
                if i == 8:
                    inverse_std(hb, HALVES + 2 * hb + 1, bk[1], eps)
                if i in (4, 8) and hb:
                    a.preload_act_table_set("exp_and_others")
                if i == 9:
                    act.wait_ge(S["tn_r"], hb + 1)
                    a.activation(tn_hi[:, hb, :], tn[:, hb, :], ACT.Copy).then_inc(S["tnh_r"], 1)
                if i == 10:
                    act.wait_ge(S["dif_r"], hb + 1)
                    a.activation(e1[:], e1[:], ACT.Exp, bias=zero).then_inc(S["ex_r"], 1)
                if i == 12:
                    act.wait_ge(S["tr_r"], BLK * (hb + 1))
                    a.activation(CE[:, hb, :], bank[bk[1]][0:64, :], ACT.Copy).then_inc(S["ceh_r"], 1)

            def round_scaled(k):
                act.wait_ge(S["xs_r"], k + 1)
                if k >= 2:
                    act.wait_ge(S["up_r"], FH * (k - 1))
                a.activation(xs_hi[:, k % 2, :], xs, ACT.Copy).then_inc(S["xsh_r"], 1)

            def gate_tanh(k, f):
                act.wait_ge(S["g_r"], FH * k + f + 1)
                if k:
                    act.wait_ge(S["hid_r"], FH * (k - 1) + f + 1)
                a.activation(th[:, f, :], bank[GATE[f]][:], ACT.Tanh, scale=0.5, bias=zero).then_inc(S["th_r"], 1)

            for k in range(SCAN1, LEAD_END):
                back(0, k - BACK_STEP)
                scan_step(k)
            a.preload_act_table_set("exp_and_others")
            round_scaled(0)
            for k in range(HALVES * E):
                for f in range(FH):
                    gate_tanh(k, f)
                    j = beside(FH * k + f)
                    if j is not None and j < STEPS:
                        scan_step(j)
                    back(1, back_item(FH * k + f))
                    if f == 0 and k + 1 < HALVES * E:
                        round_scaled(k + 1)

        @block.vector
        def _(dve):
            v = nc.vector

            def centre(hb, n, b, src):
                dve.wait_ge(S["mean_r"], n + 1)
                v.tensor_tensor(xm[:, hb, :], src, bank[b][:], ALU.subtract).then_inc(S["cen_r"], 1)

            def scale(hb, n, name="norm_r"):
                dve.wait_ge(S["rstd_r"], n + 1)
                v.tensor_tensor(xm[:, hb, :], xm[:, hb, :], sq[:, hb, :], ALU.mult).then_inc(S[name], 1)

            for hb in range(HALVES):
                centre(hb, hb, hb, X[:, hb, :])
            dve.wait_ge(S["sel1"], 4)
            v.tensor_copy(sel[:].rearrange("r s (j d) -> r s j d", j=2),
                          unit[:].rearrange("r (j s o) -> r s j o", j=2, o=1).broadcast_to([P, NS, 2, DI]))\
                .then_inc(S["sel_r"], 1)
            v.tensor_scalar(sel_e[:], unit[0:64, 0:E], 0.5, None, ALU.mult).then_inc(S["sele_r"], 1)
            dve.wait_ge(S["A_r"], 1)
            v.tensor_scalar(A[:], A[:], -1.0, None, ALU.mult).then_inc(S["A_r"], 1)
            for hb in range(HALVES):
                scale(hb, hb)
            dve.wait_ge(S["par_in"], 16)
            for hb in range(HALVES):
                dve.wait_ge(S["norm_r"], hb + 1)
                v.tensor_scalar(chk[:, hb, :], xm[:, hb, :], p("norm_g"), p("norm_b"), ALU.mult, ALU.add)\
                    .then_inc(S["chk_r"], 1)
            cw = COLS["conv_w"][0]
            for hb in range(HALVES):
                for tap in range(TAPS):
                    for gr in range(PAIRS * hb, PAIRS * (hb + 1)):
                        w = par[:, cw + TAPS - 1 - tap:cw + TAPS - tap]
                        src = bank[4 + gr][:].rearrange("p (b t) -> p b t", t=T)[:, :, 0:T - tap]
                        dst = y[:, gr, :].rearrange("p (b t) -> p b t", t=T)[:, :, tap:T]
                        if tap == 0:
                            dve.wait_ge(S["xi_r"], gr + 1)
                            v.tensor_scalar(dst, src, w, None, ALU.mult).then_inc(S["conv_r"], 1)
                        else:
                            dve.wait_ge(S["conv_r"], (TAPS * hb + tap - 1) * PAIRS + gr % PAIRS + 1)
                            v.scalar_tensor_tensor(dst, src, w, dst, ALU.mult, ALU.add).then_inc(S["conv_r"], 1)

            def bc_rest(gr):
                dve.wait_ge(S["bch_r"], gr + 1)
                v.scalar_tensor_tensor(BC[:, gr, :], BC[:, gr, :].bitcast(F32), rest_row, bank[4 + gr][:],
                                       ALU.mult, ALU.add).then_inc(S["bcl_r"], 1)

            def square_z(gr):
                dve.wait_ge(S["lz_r"], gr + 1)
                v.tensor_tensor(lw[:, gr, :], dt[:, gr, :], dt[:, gr, :], ALU.mult).then_inc(S["lw_r"], 1)

            def softplus(gr, i):
                if i == 0:
                    dve.wait_ge(S["lw_r"], gr + 1)
                    v.tensor_scalar(lr[:, gr, :], lw[:, gr, :], LOG1P[4], LOG1P[3], ALU.mult, ALU.add)\
                        .then_inc(S["lq_r"], 1)
                elif i < 4:
                    dve.wait_ge(S["lq_r"], 4 * gr + i)
                    v.scalar_tensor_tensor(lr[:, gr, :], lr[:, gr, :], 0.0 if i == 1 else LOG1P[4 - i], lw[:, gr, :],
                                           ALU.add, ALU.mult).then_inc(S["lq_r"], 1)
                elif i == 4:
                    dve.wait_ge(S["lq_r"], 4 * gr + 4)
                    v.scalar_tensor_tensor(lr[:, gr, :], lr[:, gr, :], LOG1P[0], dt[:, gr, :], ALU.add, ALU.mult)\
                        .then_inc(S["lp_r"], 1)
                else:
                    dve.wait_ge(S["lp_r"], gr + 1)
                    v.scalar_tensor_tensor(dt[:, gr, :], bank[dt_bank(gr)][:], 0.0, lr[:, gr, :], ALU.max, ALU.add)\
                        .then_inc(S["dt_r"], 1)

            dve.wait_ge(S["rest0"], 3)
            def round_weights(c):
                dve.wait_ge(S[f"w_in{c}"], 16)
                w, es = c * WCH // E, slice(c * WCH % E, c * WCH % E + WCH)
                v.tensor_copy(W_hi[w][:, es], stage(c)).then_inc(S["w_hi2"], 1)

            for c in range(ACT_ROUNDS, STAGES + 4):
                round_weights(c)
            for gr in (0, 1):
                bc_rest(gr)
            for c in range(STAGES + 4, CHUNKS_W - 4):
                round_weights(c)
            square_z(0)
            for i in range(6):
                softplus(0, i)
                if i in (0, 1):
                    bc_rest(2 + i)
            for c in range(CHUNKS_W - 4, CHUNKS_W):
                round_weights(c)
            for gr in range(1, GROUPS):
                square_z(gr)
            dve.wait_ge(S["w_lo"], CHUNKS_W)

            def scan(k):
                dve.wait_ge(S["dA_r"], k + 1)
                dve.wait_ge(S["u_r"], k + 1)
                if k >= 2:
                    dve.wait_ge(S["hc_r"], k - 1)
                for b in range(2):
                    t = slice(b * T, (b + 1) * T)
                    v.tensor_tensor_scan(h[:, k % 2, t], dA[:, k % 3, t], u[:, k % 3, t], 0.0,
                                         ALU.mult, ALU.add).then_inc(S["scan_r"], 1)

            def weigh(k):
                dve.wait_ge(S["pC"], k + 1)
                dve.wait_ge(S["scan_r"], 2 * (k + 1))
                if k >= 3:
                    dve.wait_ge(S["red_r"], min(k - 2, POOL0))
                if k - 3 > POOL0:
                    dve.wait_ge(S["acc_r"], acc_count(k - 2))
                dst = y[:, k // NS, :] if k == POOL0 else hc[:, k % 3]
                v.tensor_tensor(dst, h[:, k % 2], bank[c_bank(k)][:], ALU.mult).then_inc(S["hc_r"], 1)

            def finish_group(gr):
                if gr < GROUPS - 1:
                    dve.wait_ge(S["red_r"], NS * (gr + 1))
                    total = bank[STATE_SUM[gr]][:]
                else:
                    dve.wait_ge(S["acc_r"], acc_count(STEPS))
                    total = y[:, gr, :]
                v.scalar_tensor_tensor(y[:, gr, :], xc[:, gr, :], p("D"), total, ALU.mult, ALU.add)\
                    .then_inc(S["yg_r"], 1)
                dve.wait_ge(S["yg_r"], gr + 1)
                v.tensor_tensor(y[:, gr, :], y[:, gr, :], zs[:, gr, :], ALU.mult).then_inc(S["y_r"], 1)

            def back(hb, i):
                bk = BACK[hb]
                if i == 0:
                    finish_group(PAIRS * hb + 1)
                if i == 1:
                    dve.wait_ge(S["op_r"], hb + 1)
                    v.scalar_tensor_tensor(chk[:, hb, :], chk[:, hb, :], p("skip"), bank[bk[0]][:], ALU.mult, ALU.add)\
                        .then_inc(S["y2_r"], 1)
                if i == 2:
                    centre(hb, HALVES + 2 * hb, bk[1], chk[:, hb, :])
                if i == 4:
                    scale(hb, HALVES + 2 * hb)
                    dve.wait_ge(S["norm_r"], HALVES + hb + 1)
                    v.tensor_scalar(chk[:, hb, :], xm[:, hb, :], p("norm_g"), p("norm_b"), ALU.mult, ALU.add)\
                        .then_inc(S["y3_r"], 1)
                if i == 5:
                    dve.wait_ge(S["pj_r"], hb + 1)
                    v.scalar_tensor_tensor(X[:, hb, :], bank[bk[1]][:], p("proj_b"), X[:, hb, :], ALU.add, ALU.add)\
                        .then_inc(S["x1_r"], 1)
                if i == 6:
                    centre(hb, HALVES + 2 * hb + 1, bk[0], X[:, hb, :])
                if i == 8:
                    scale(hb, HALVES + 2 * hb + 1, "tn_r")
                if i == 9:
                    dve.wait_ge(S["tnh_r"], hb + 1)
                    v.tensor_tensor(tn_lo[:, hb, :], tn[:, hb, :], tn_hi[:, hb, :].bitcast(F32), ALU.subtract)\
                        .then_inc(S["tnl_r"], 1)
                if i == 9:
                    dve.wait_ge(S["lg_r"], hb + 1)
                    v.tensor_copy(L[:].rearrange("p b e -> p (b e)"), bank[bk[0]][:, 0:BLK * E]).then_inc(S["L_r"], 1)
                    dve.wait_ge(S["L_r"], hb + 1)
                    for b in range(BLK):
                        v.max(top[:, b, :], L[:, b, :]).then_inc(S["top_r"], 1)
                    for b in range(BLK):
                        dve.wait_ge(S["top_r"], BLK * hb + b + 1)
                        v.max_index(topi[:, b, :], top[:, b, :], L[:, b, :]).then_inc(S["topi_r"], 1)
                    v.tensor_tensor(e1[:], top[:, :, 1:2], top[:, :, 0:1], ALU.subtract).then_inc(S["dif_r"], 1)
                    dve.wait_ge(S["topi_r"], BLK * (hb + 1))
                    v.tensor_copy(topf[:], topi[:, :, 0:2]).then_inc(S["topf_r"], 1)
                if i == 10:
                    dve.wait_ge(S["topf_r"], hb + 1)
                    for j in range(2):
                        v.tensor_tensor(oh[:, j], iota_e[:], topf[:, :, j:j + 1].broadcast_to([P, BLK, E]),
                                        ALU.is_equal).then_inc(S["eq_r"], 1)
                    dve.wait_ge(S["ex_r"], hb + 1)
                    v.tensor_scalar(w01[:, :, 0:1], e1[:], 1.0, None, ALU.add).then_inc(S["sum_r"], 1)
                    dve.wait_ge(S["sum_r"], hb + 1)
                    v.reciprocal(w01[:, :, 0:1], w01[:, :, 0:1]).then_inc(S["w0_r"], 1)
                    dve.wait_ge(S["w0_r"], hb + 1)
                    v.tensor_tensor(w01[:, :, 1:2], e1[:], w01[:, :, 0:1], ALU.mult).then_inc(S["w1_r"], 1)
                    dve.wait_ge(S["w1_r"], hb + 1)
                    for j in range(2):
                        dve.wait_ge(S["eq_r"], 2 * hb + j + 1)
                        v.tensor_tensor(oh[:, j], oh[:, j], w01[:, :, j:j + 1].broadcast_to([P, BLK, E]), ALU.mult)\
                            .then_inc(S["ow_r"], 1)
                    dve.wait_ge(S["ow_r"], 2 * hb + 2)
                    for part in range(2):
                        v.tensor_tensor(cpad[:, :, 32 * part:32 * part + E], oh[:, 0], oh[:, 1], ALU.add)\
                            .then_inc(S["ce_r"], 1)
                if i == 12:
                    dve.wait_ge(S["ceh_r"], hb + 1)
                    v.tensor_tensor(CE[32:64, hb, :], bank[bk[1]][32:64, :], CE[32:64, hb, :].bitcast(F32),
                                    ALU.subtract).then_inc(S["cel_r"], 1)

            def scale_tokens(k):
                dve.wait_ge(S["ceb_r"], k + 1)
                if k:
                    dve.wait_ge(S["xsl_r"], k)
                v.tensor_tensor(xs, tn[:, k // E, :], bank[SPREAD][:], ALU.mult).then_inc(S["xs_r"], 1)

            def gate(k, f):
                dve.wait_ge(S["th_r"], FH * k + f + 1)
                v.scalar_tensor_tensor(th[:, f, :], th[:, f, :], 1.0, bank[GATE[f]][:], ALU.add, ALU.mult)\
                    .then_inc(S["m_r"], 1)

            def result(hb):
                dve.wait_ge(S["yd_r"], (hb + 1) * E * FH)
                v.tensor_tensor(X[:, hb, :], X[:, hb, :], bank[YSUM][:], ALU.add).then_inc(S["res_r"], 1)

            def hidden(k, f):
                dve.wait_ge(S["up_r"], FH * k + f + 1)
                dve.wait_ge(S["m_r"], FH * k + f + 1)
                if k >= 2:
                    dve.wait_ge(S["yd_r"], FH * (k - 2) + f + 1)
                v.tensor_tensor(hid[k % 2][:, f, :], th[:, f, :], bank[UP[f]][:], ALU.mult).then_inc(S["hid_r"], 1)

            for k in range(SCAN0, SCAN1):
                scan(k)
                if k:
                    weigh(k - 1)
                if k // 6 + 1 < GROUPS:
                    softplus(k // 6 + 1, k % 6)
                if k == NS + 3:
                    finish_group(0)
            for k in range(SCAN1, LEAD_END):
                scan(k)
                weigh(k - 1)
                back(0, k - BACK_STEP)
            weigh(LEAD_END - 1)
            finish_group(2)
            scale_tokens(0)
            for k in range(HALVES * E):
                for f in range(FH):
                    gate(k, f)
                    if f == 0 and k + 1 < HALVES * E:
                        scale_tokens(k + 1)
                    j = beside(FH * k + f)
                    if j is not None and j < STEPS:
                        scan(j)
                    hidden(k, f)
                    if j is not None and j > LEAD_END:
                        weigh(j - 1)
                    back(1, back_item(FH * k + f))
                if k == E:
                    result(0)
            result(1)

        @block.tensor
        def _(pe):
            t = nc.tensor
            pe.wait_ge(S["const0"], 2)

            def mm(o, w, r, name, start=True, stop=True):
                return t.matmul(o, w, r, start=start, stop=stop).then_inc(S[name], 1)

            def mean(b, src):
                mm(bank[b][:], mean_w[:], src, "mean_r")

            def variance(hb, n, b, w):
                pe.wait_ge(S["sq_r"], n + 1)
                mm(bank[b][:], w[:], sq[:, hb, :], "var_r")

            def keep_warm(count, b=7):
                for _ in range(count):
                    t.matmul(bank[b][:, 0:P], mean_w[:], mean_w[:], start=True, stop=True)

            keep_warm(12)
            for hb in range(HALVES):
                pe.wait_ge(S[f"x_in{hb}"], 16)
                mean(hb, X[:, hb, :])
            for hb in range(HALVES):
                variance(hb, hb, 2 + hb, var_in_w)
            keep_warm(12)
            pe.wait_ge(S["par_in"], 16)
            for hb in range(HALVES):
                pe.wait_ge(S["chk_r"], hb + 1)
                for q in range(PAIRS):
                    rows = slice(64 * q, 64 * q + 64)
                    mm(bank[4 + 2 * hb + q][:], p("in_x")[rows], chk[rows, hb, :], "xi_r")
                if hb == 0:
                    pe.wait_ge(S["cen_r"], HALVES)
                    pe.wait_ge(S["ln_r"], HALVES)
                for q in range(PAIRS):
                    rows = slice(64 * q, 64 * q + 64)
                    mm(bank[2 * hb + q][:], p("in_z")[rows], chk[rows, hb, :], "z_r")

            def project_dt(gr):
                pe.wait_ge(S["dtr_r"], gr + 1)
                if gr:
                    pe.wait_ge(S["bcl_r"], gr)
                mm(bank[dt_bank(gr)][:], p("dt_out")[0:DTK], dtr[:, gr, :], "dtp_r")

            for hb in range(HALVES):
                for gr in range(PAIRS * hb, PAIRS * (hb + 1)):
                    pe.wait_ge(S["xc_r"], gr + 1)
                    pe.wait_ge(S["zs_r"], gr + 1)
                    mm(bank[gr][0:2 * RANK, :], p("dt_in"), xc[:, gr, :], "dtraw_r")
                    mm(bank[4 + gr][:], p("bc"), xc[:, gr, :], "bc_r")
                if hb == 0:
                    pe.wait_ge(S["zs_r"], GROUPS)
                    keep_warm(12, 3)
                for gr in range(PAIRS * hb, PAIRS * (hb + 1)):
                    project_dt(gr)
            pe.wait_ge(S["sel_r"], 1)
            pe.wait_ge(S["ident_r"], 1)
            pe.wait_ge(S["bcl_r"], GROUPS)
            keep_warm(4)

            def sum_state(k):
                gr, s = divmod(k, NS)
                if k == 2 * NS:
                    pe.wait_ge(S["yg_r"], 1)
                elif k == NS:
                    pe.wait_ge(S["dt_r"], GROUPS)
                pe.wait_ge(S["hc_r"], k + 1)
                mm(bank[STATE_SUM[gr]][:], ident[:], hc[:, k % 3], "red_r", s == 0, s == NS - 1)

            def spread_b(k, idle=0):
                if before(b_bank, k):
                    pe.wait_ge(S["Bs_r"], before(b_bank, k))
                keep_warm(idle, b_bank(k))
                mm(bank[b_bank(k)][:], sel[0:64, k % NS, :], BC[0:64, k // NS, :], "pB")

            def spread_c(k):
                if before(c_bank, k):
                    pe.wait_ge(S["hc_r"], before(c_bank, k))
                mm(bank[c_bank(k)][:], sel[64:128, k % NS, :], BC[64:128, k // NS, :], "pC")

            for k in range(3):
                spread_b(k, 4)
            spread_c(0)
            pe.wait_ge(S["dt_r"], 1)
            keep_warm(6, 0)
            for k in range(SCAN0, SCAN1):
                spread_b(k + 3, 2 if k < WARM_STEPS else 0)
                if k + 1 < SCAN1:
                    spread_c(k + 1)
                if k >= 2:
                    sum_state(k - 2)

            def back(hb, i):
                bk = BACK[hb]
                if i == 1:
                    for q in range(PAIRS):
                        pe.wait_ge(S["y_r"], 2 * hb + q + 1)
                        o = t.matmul(bank[bk[0]][64 * q:64 * q + 64, :], p("out"), y[:, 2 * hb + q, :],
                                     start=True, stop=True)
                    o.then_inc(S["op_r"], 1)
                if i == 2:
                    pe.wait_ge(S["y2_r"], hb + 1)
                    mean(bk[1], chk[:, hb, :])
                if i == 3:
                    variance(hb, HALVES + 2 * hb, bk[0], mean_w)
                if i == 5:
                    pe.wait_ge(S["y3_r"], hb + 1)
                    mm(bank[bk[1]][:], p("proj"), chk[:, hb, :], "pj_r")
                if i == 6:
                    pe.wait_ge(S["x1_r"], hb + 1)
                    mean(bk[0], X[:, hb, :])
                if i == 7:
                    variance(hb, HALVES + 2 * hb + 1, bk[1], mean_w)
                if i == 9:
                    pe.wait_ge(S["tn_r"], hb + 1)
                    for b in range(BLK):
                        o = t.matmul(bank[bk[0]][:, b * E:(b + 1) * E], tn[:, hb, b * P:(b + 1) * P], p("router"),
                                     start=True, stop=True)
                    o.then_inc(S["lg_r"], 1)
                if i == 11:
                    pe.wait_ge(S["ce_r"], 2 * (hb + 1))
                    for b in range(BLK):
                        t.transpose(bank[bk[1]][0:64, b * P:(b + 1) * P], cpad[:, b, :], ident[:])\
                            .then_inc(S["tr_r"], 1)

            def spread_gate(k):
                pe.wait_ge(S["cel_r"], k // E + 1)
                if k:
                    pe.wait_ge(S["xs_r"], k)
                mm(bank[SPREAD][:], sel_e[:, k % E:k % E + 1].broadcast_to([P // 2, P]), CE[:, k // E, :], "ceb_r")

            def product(b, w, k, f, hi, lo, name):
                ws = slice(f * P, (f + 1) * P)
                t.matmul(bank[b][:], W_hi[w][:, k % E, ws], hi, start=True, stop=False)
                t.matmul(bank[b][:], W_hi[w][:, k % E, ws], lo, start=False, stop=False)
                mm(bank[b][:], W_lo[w][:, k % E, ws], hi, name, False, True)

            def down(k, f):
                pe.wait_ge(S["hid_r"], FH * k + f + 1)
                e = k % E
                if e == 0 and f == 0 and k:
                    pe.wait_ge(S["res_r"], k // E)
                mm(bank[YSUM][:], Wd[:, e, f, :], hid[k % 2][:, f, :], "yd_r",
                   e == 0 and f == 0, e == E - 1 and f == FH - 1)

            for k in range(SCAN1, LEAD_END):
                if k - BACK_STEP not in (3, 7):
                    back(0, k - BACK_STEP)
                spread_b(k + 3)
                spread_c(k)
                if k - 2 < POOL0:
                    sum_state(k - 2)
                if k - BACK_STEP in (3, 7):
                    back(0, k - BACK_STEP)
            for k in range(LEAD_END - 2, POOL0):
                sum_state(k)
            pe.wait_ge(S["sele_r"], 1)
            pe.wait_ge(S["wd_in"], 16)
            pe.wait_ge(S["w_lo"], CHUNKS_W)
            pe.wait_ge(S["yg_r"], 3)
            pe.wait_ge(S["Bs_r"], LEAD_END)
            pe.wait_ge(S["hc_r"], LEAD_END)
            spread_gate(0)
            for k in range(HALVES * E):
                hb = k // E
                for f in range(FH):
                    slot = FH * k + f
                    if f == 0:
                        if k + 1 < HALVES * E:
                            spread_gate(k + 1)
                        pe.wait_ge(S["tnl_r"], hb + 1)
                    if slot >= FH:
                        pe.wait_ge(S["m_r"], slot - 1)
                    product(GATE[f], 0, k, f, tn_hi[:, hb, :], tn_lo[:, hb, :], "g_r")
                    if back_item(slot - 1) in (3, 7):
                        back(1, back_item(slot - 1))
                    j = beside(slot)
                    if j is not None:
                        if j + 3 < STEPS:
                            spread_b(j + 3)
                    if f == 0:
                        pe.wait_ge(S["xsl_r"], k + 1)
                    if slot >= FH:
                        pe.wait_ge(S["hid_r"], slot - 1)
                    product(UP[f], 1, k, f, xs_hi[:, k % 2, :], xs_lo[:, k % 2, :], "up_r")
                    if j is not None and j > LEAD_END:
                        spread_c(j - 1)
                    if k:
                        down(k - 1, f)
                    if back_item(slot) not in (3, 7):
                        back(1, back_item(slot))
            for f in range(FH):
                down(HALVES * E - 1, f)


def kernel(**inputs):
    import concourse.bacc as bacc
    from concourse.bass_utils import run_bass_kernel_spmd as run

    a = {k.removeprefix("L0_"): np.asarray(v) for k, v in inputs.items()}
    par = np.zeros((P, NPACK), np.float32)

    def put(name, m, row=0, col=0):
        c0 = COLS[name][0] + col
        par[row:row + m.shape[0], c0:c0 + m.shape[1]] = m

    put("norm_g", a["conv_norm_g"][:, None])
    put("norm_b", a["conv_norm_b"][:, None])
    put("proj_b", a["conv_proj_b"][:, None])
    put("skip", np.broadcast_to(a["conv_skip_scale"][:, None], (P, 1)))
    put("proj", a["conv_proj_w"].T)
    put("router", a["ffn_router_w"].T)
    for j in range(2):
        for name, key in (("conv_b", "conv_conv_b"), ("D", "conv_D_param")):
            put(name, a[key][:, None], DI * j)
        put("conv_w", a["conv_conv_w"], DI * j)
        put("A_log", a["conv_A_log"], DI * j)
        put("dt_in", a["conv_x_proj_w"].T[:, 0:RANK], DI * j, RANK * j)
        put("dt_out", a["conv_dt_proj_w"].T, RANK * j, DI * j)
        put("dt_out", a["conv_dt_proj_b"][None, :], 2 * RANK, DI * j)
        put("out", a["conv_out_proj_w"].T, DI * j, DM * j)
        for part in range(2):
            for i in range(2):
                put("bc", a["conv_x_proj_w"].T[:, RANK + NS * i:RANK + NS * (i + 1)], DI * j, 64 * i + 32 * part + NS * j)
    for q in range(CHUNKS):
        put("in_x", a["conv_in_proj_w"].T[:, 0:DI], DM * q, DI * (q % 2))
        put("in_z", a["conv_in_proj_w"].T[:, DI:2 * DI], DM * q, DI * (q % 2))
    arrays = {"x": np.ascontiguousarray(a["x"].reshape(BATCH, C, T)), "params": par, "gate_w": a["ffn_gate_w"],
              "up_w": a["ffn_up_w"], "down_w": a["ffn_down_w"]}

    nc = bacc.Bacc("TRN2", target_bir_lowering=False, num_devices=1)
    args = [nc.dram_tensor(k, v.shape, F32, kind="ExternalInput").ap() for k, v in arrays.items()]
    out = nc.dram_tensor("out", (BATCH, C, T), F32, kind="ExternalOutput").ap()
    build(nc, *args, out)
    r = run(nc, [arrays], core_ids=[0])
    return r.results[0]["out"].reshape(BATCH, C, 16, 16)
```

```python
from contextlib import ExitStack

import numpy as np
import concourse.bass as bass
from concourse import mybir

P = 128
BATCH, C, T = 4, 128, 256
CHUNKS, DM, DI = 4, 32, 64
PAIRS = CHUNKS // 2
NS = 16
RANK = 2
TAPS = 4
E, F = 16, 256
FH = F // P
HALVES = 2
N = BATCH * T // HALVES
GROUPS = HALVES * PAIRS
DTK = 2 * RANK + 1
LN2 = float(np.log(2.0))
LOG1P = (2.00000001, 0.66666317, 0.40024839, 0.27961494, 0.28174741)
BLK = N // P
EPS_IN, EPS = 1e-6, 1e-5
WCH = 2
CHUNKS_W = 2 * E // WCH
SCAN0, SCAN1 = 0, PAIRS * NS
STEPS = GROUPS * NS
POOL0 = 3 * NS
LEAD_END = POOL0 + 2
SCAN_SLOTS = 14
STAGES = 8
ACT_ROUNDS = 4
BACK_STEP = SCAN1 + 1
LAST_RESTS = 4
WARM_STEPS = 8
BACK_PE = {1: 1, 2: 2, 3: 3, 6: 5, 7: 6, 8: 7, 11: 9, 13: 11}
BACK_ACT = {3: 3, 4: 4, 8: 7, 9: 8, 11: 9, 12: 10, 14: 12}
BACK_DVE = {0: 0, 1: 1, 2: 2, 5: 4, 6: 5, 7: 6, 10: 8, 11: 9, 12: 10, 14: 12}
LATE = (3, 7, 11)
ITEMS = 13

F32, F32R, U32 = mybir.dt.float32, mybir.dt.float32r, mybir.dt.uint32
ALU, ACT = mybir.AluOpType, mybir.ActivationFunctionType

COLS = {}
_at = 0
for _name, _width in (("norm_g", 1), ("norm_b", 1), ("proj_b", 1), ("skip", 1), ("conv_w", TAPS), ("conv_b", 1),
                      ("D", 1), ("A_log", NS), ("in_x", P), ("in_z", P), ("bc", P), ("dt_in", 2 * RANK),
                      ("dt_out", P), ("out", 2 * DM), ("proj", P), ("router", E)):
    COLS[_name] = (_at, _at + _width)
    _at += _width
NPACK = _at


def build(nc, x, params, gate_w, up_w, down_w, out):
    with ExitStack() as ctx:
        def sb(name, shape, dt=F32):
            return ctx.enter_context(nc.sbuf_tensor(name, shape, dt))

        bank = [ctx.enter_context(nc.psum_tensor(f"bank{i}", [P, N], F32)) for i in range(8)]
        STATE_SUM = (7, 6, 6)
        BACK = ((4, 5), (2, 3))
        YSUM, SPREAD = 6, 7
        GATE, UP = (4, 0), (5, 1)

        def b_bank(k):
            return (2, 1)[k % 2] if k < LEAD_END else 2

        def c_bank(k):
            return (3, 0)[k % 2] if k < LEAD_END else 3

        def dt_bank(gr):
            return 3 + gr if gr else 0

        def before(bank_of, k):
            return max((j + 1 for j in range(k) if bank_of(j) == bank_of(k)), default=0)

        X = sb("X", [P, HALVES, N])
        par = sb("par", [P, NPACK])
        W_hi = [sb("Wg_hi", [P, E, F], F32R), sb("Wu_hi", [P, E, F], F32R)]
        W_lo = [sb("Wg_lo", [P, E, F], F32R), sb("Wu_lo", [P, E, F], F32R)]
        Wd = sb("Wd", [P, E, FH, C])
        mean_w = sb("mean_w", [P, P])
        cst = sb("cst", [P, 5])
        ident = sb("ident", [P, P])
        iota_e = sb("iota_e", [P, BLK, E])
        sel = sb("sel", [P, NS, P], F32R)
        sel_e = sb("sel_e", [P // 2, E], F32R)
        A = sb("A", [P, NS])
        xm = sb("xm", [P, HALVES, N])
        sq = sb("sq", [P, HALVES, N])
        chk = sb("chk", [P, HALVES, N])
        xc = sb("xc", [P, GROUPS, N])
        zs = sb("zs", [P, GROUPS, N])
        dt = sb("dt", [P, GROUPS, N])
        y = sb("y", [P, GROUPS, N])
        top = sb("top", [P, BLK, 8])
        topi = sb("topi", [P, BLK, 8], U32)
        topf = sb("topf", [P, BLK, 2])
        w01 = sb("w01", [P, BLK, 2])
        e1 = sb("e1", [P, BLK, 1])
        cpad = sb("cpad", [P, BLK, P // 2])
        CE = sb("CE", [P // 2, HALVES, N], F32R)
        tn_hi = sb("tn_hi", [P, HALVES, N], F32R)
        tn_lo = sb("tn_lo", [P, HALVES, N], F32R)
        xs_hi = sb("xs_hi", [P, 2, N], F32R)
        xs_lo = sb("xs_lo", [P, 2, N], F32R)
        with ExitStack() as scan_ctx:
            def scan_sb(name, shape, dt=F32):
                return scan_ctx.enter_context(nc.sbuf_tensor(name, shape, dt))
            ring = scan_sb("ring", [P, 5 * 3, N])
            dtx = scan_sb("dtx", [P, GROUPS, N])
            BC = scan_sb("BC", [P, GROUPS, N], F32R)
        u, Bs, h, hc, dA = (ring[:, 3 * i:3 * i + 3] for i in range(5))
        Wd_hi = sb("Wd_hi", [P, E, FH, C], F32R)
        Wd_lo = sb("Wd_lo", [P, E, FH, C], F32R)
        hid_hi = sb("hid_hi", [P, 3, N], F32R)
        hid_lo = sb("hid_lo", [P, 3, N], F32R)
        xs = xc[:, 0, :]
        th = dt[:, 0:FH]
        hid = (y[:, 0:FH], zs[:, 0:FH])
        var_in_w = xc[:, 0, 0:P]
        unit = xc[:, 1, 0:32]
        L = [chk[:, hb, 0:BLK * E].rearrange("p (b e) -> p b e", e=E) for hb in range(HALVES)]
        oh = [chk[:, hb, BLK * E:3 * BLK * E].rearrange("p (j b e) -> p j b e", j=2, e=E) for hb in range(HALVES)]
        tn = xm
        dtr = ring[0:DTK, 5:5 + GROUPS]
        lr = y
        lw = dtx
        stages = [ring[:, 9 + i] for i in range(4)] + [b[:, hb] for b in (sq, xm) for hb in range(HALVES)]

        def stage(c):
            return stages[c % STAGES].rearrange("p (e f) -> p e f", f=F)

        def weight_chunk(c):
            return c * WCH // E, slice(c * WCH % E, c * WCH % E + WCH)

        eps_in, eps, zero, mln2, rest_row = (cst[:, i:i + 1] for i in range(5))

        def p(name):
            a, b = COLS[name]
            return par[:, a:b]

        names = ("x_in0 x_in1 par_in wd_in const0 const1 ident_r sel0 sel1 sel_r sele_r A_r cen_r sq_r mean_r "
                 "var_r ln_r rstd_r norm_r chk_r xi_r z_r tap0_r conv_r xc_r zs_r bc_r dtraw_r dtr_r dtp_r bch_r "
                 "bcl_r abs_r lz_r lw_r lq_r lp_r dt_r dtx_r pB pC Bs_r dA_r u_r scan_r hc_r red_r acc_r yg_r y_r "
                 "op_r y2_r y3_r pj_r x1_r tn_r tnh_r tnl_r lg_r L_r top_r topi_r topf_r dif_r ex_r sum_r w0_r "
                 "w1_r eq_r ow_r ce_r tr_r ceh_r cel_r ceb_r xs_r xsh_r xsl_r g_r up_r th_r m_r hid_r yd_r res_r "
                 "out_d w_hi w_hi2 w_lo wd_hi wd_lo hidh_r hidl_r rest0").split()
        names += [f"w_in{c}" for c in range(CHUNKS_W)]
        S = {n: ctx.enter_context(nc.semaphore(n)) for n in names}

        def acc_count(k):
            return sum(1 for i in range(POOL0, k) if i % NS)

        step_at = {t * SCAN_SLOTS // (STEPS - LEAD_END): LEAD_END + t for t in range(STEPS - LEAD_END)}
        step_at[SCAN_SLOTS] = STEPS

        def beside(slot):
            return step_at.get(slot)

        def down_in_parts(slot):
            return FH * E <= slot < FH * (HALVES * E - 1)

        def down_chunk(slot):
            i = slot - SCAN_SLOTS - 3
            return i if i in range(E // 2) else None

        def back_item(slot):
            i = slot - SCAN_SLOTS - 1
            return i if i in range(ITEMS) and slot < FH * E else None

        block = ctx.enter_context(nc.Block())

        @block.sync
        def _(sp):
            for hb in range(HALVES):
                sp.dma_start(X[:, hb, :].rearrange("p (b t) -> p b t", t=T),
                             x[2 * hb:2 * hb + 2].rearrange("b c t -> c b t")).then_inc(S[f"x_in{hb}"], 16)
            for c in range(CHUNKS_W):
                if c >= STAGES:
                    sp.wait_ge(S["w_lo"], c - STAGES + 1)
                elif c >= STAGES - HALVES:
                    sp.wait_ge(S["chk_r"], c - (STAGES - HALVES) + 1)
                elif c >= STAGES - 2 * HALVES:
                    sp.wait_ge(S["norm_r"], c - (STAGES - 2 * HALVES) + 1)
                w, es = weight_chunk(c)
                sp.dma_start(stage(c), (gate_w, up_w)[w][es].rearrange("e h f -> h e f"))\
                    .then_inc(S[f"w_in{c}"], 16)
                if c == STAGES - 1:
                    sp.dma_start(Wd[:], down_w.rearrange("e (f p) h -> p e f h", p=P)).then_inc(S["wd_in"], 16)
            for hb in range(HALVES):
                sp.wait_ge(S["res_r"], hb + 1)
                sp.dma_start(out[2 * hb:2 * hb + 2].rearrange("b c t -> c b t"),
                             X[:, hb, :].rearrange("p (b t) -> p b t", t=T)).then_inc(S["out_d"], 16)
            sp.wait_ge(S["out_d"], 16 * HALVES)

        @block.gpsimd
        def _(pool):
            g = nc.gpsimd
            g.memset(mean_w[:], 1.0 / C).then_inc(S["const0"], 1)
            g.memset(var_in_w, (1.0 + EPS) / C).then_inc(S["const0"], 1)
            for i, value in enumerate((EPS_IN * EPS, EPS, 0.0, -LN2)):
                g.memset(cst[:, i:i + 1], value).then_inc(S["const0"], 1)
            g.memset(rest_row, 0.0).then_inc(S["rest0"], 1)
            for row in (32, 96):
                pool.wait_ge(S["rest0"], 1 + row // 96)
                g.memset(cst[row:row + 32, 4:5], -1.0).then_inc(S["rest0"], 1)
            pool.wait_ge(S["rest0"], 3)
            g.memset(unit, 0.0).then_inc(S["sel0"], 1)
            pool.wait_ge(S["sel0"], 1)
            for q in range(4):
                v = unit[32 * q:32 * q + 32, :]
                g.affine_select(out=v, in_=v, compare_op=ALU.not_equal, fill=1.0, base=0,
                                pattern=[[-1, 32]], channel_multiplier=1).then_inc(S["sel1"], 1)
            pool.wait_ge(S["sel1"], 4)
            g.memset(dtr, 1.0).then_inc(S["const1"], 1)
            g.memset(cpad[:], 0.0).then_inc(S["const1"], 1)
            g.iota(iota_e[:], pattern=[[0, BLK], [1, E]], base=0, channel_multiplier=0,
                   allow_small_or_imprecise_dtypes=True).then_inc(S["const1"], 1)
            g.memset(ident[:], 0.0).then_inc(S["sel0"], 1)
            pool.wait_ge(S["sel0"], 2)
            g.affine_select(out=ident[:], in_=ident[:], compare_op=ALU.not_equal, fill=1.0, base=0,
                            pattern=[[-1, P]], channel_multiplier=1).then_inc(S["ident_r"], 1)

            def split_rest(c):
                if c < ACT_ROUNDS:
                    pool.wait_ge(S["w_hi"], c + 1)
                else:
                    pool.wait_ge(S["w_hi2"], c - ACT_ROUNDS + 1)
                w, es = weight_chunk(c)
                g.tensor_tensor(W_lo[w][:, es], stage(c), W_hi[w][:, es].bitcast(F32), ALU.subtract)\
                    .then_inc(S["w_lo"], 1)

            for c in range(CHUNKS_W - LAST_RESTS):
                split_rest(c)

            def scan_source(gr):
                pool.wait_ge(S["dt_r"], gr + 1)
                g.tensor_tensor(dtx[:, gr, :], dt[:, gr, :], xc[:, gr, :], ALU.mult).then_inc(S["dtx_r"], 1)

            def scan_input(k):
                pool.wait_ge(S["Bs_r"], k + 1)
                if k >= 3:
                    pool.wait_ge(S["scan_r"], 2 * (k - 2))
                g.tensor_tensor(u[:, k % 3], dtx[:, k // NS, :], Bs[:, k % 3], ALU.mult).then_inc(S["u_r"], 1)

            def add_state(k):
                if k > POOL0:
                    pool.wait_ge(S["hc_r"], k + 1)
                    pool.wait_ge(S["acc_r"], acc_count(k))
                    g.tensor_tensor(y[:, k // NS, :], y[:, k // NS, :], hc[:, k % 3], ALU.add).then_inc(S["acc_r"], 1)

            def split_scaled(k):
                pool.wait_ge(S["xsh_r"], k + 1)
                if k >= 2:
                    pool.wait_ge(S["up_r"], FH * (k - 1))
                g.tensor_tensor(xs_lo[:, k % 2, :], xs, xs_hi[:, k % 2, :].bitcast(F32), ALU.subtract)\
                    .then_inc(S["xsl_r"], 1)

            scan_source(0)
            for k in range(SCAN0, LEAD_END + 1):
                if k % NS == 0:
                    pool.wait_ge(S["dtx_r"], k // NS + 1)
                scan_input(k)
                if k % 6 == 2 and k // 6 in range(1, GROUPS):
                    scan_source(k // 6)
                if k - 2 in range(LAST_RESTS):
                    split_rest(CHUNKS_W - LAST_RESTS + k - 2)
                add_state(k - 2)
            split_scaled(0)
            for slot in range(FH * E):
                k = beside(slot)
                if k is not None and k + 1 < STEPS:
                    scan_input(k + 1)
                if slot % FH == 0:
                    split_scaled(slot // FH + 1)
                if k is not None:
                    add_state(k - 1)
                c = down_chunk(slot)
                if c is not None:
                    pool.wait_ge(S["wd_hi"], c + 1)
                    es = slice(2 * c, 2 * c + 2)
                    g.tensor_tensor(Wd_lo[:, es], Wd[:, es], Wd_hi[:, es].bitcast(F32), ALU.subtract)\
                        .then_inc(S["wd_lo"], 1)

            def split_hidden(k, f):
                pool.wait_ge(S["hidh_r"], FH * (k - E) + f + 1)
                i = (FH * k + f) % 3
                g.tensor_tensor(hid_lo[:, i], hid[k % 2][:, f, :], hid_hi[:, i].bitcast(F32),
                                ALU.subtract).then_inc(S["hidl_r"], 1)

            for k in range(E, HALVES * E):
                for f in range(FH):
                    slot = FH * k + f
                    if down_in_parts(slot - 1):
                        split_hidden((slot - 1) // FH, (slot - 1) % FH)
                    if f == 0 and k + 1 < HALVES * E:
                        split_scaled(k + 1)

        @block.scalar
        def _(act):
            a = nc.scalar
            act.dma_start(par[:], params).then_inc(S["par_in"], 16)
            a.preload_act_table_set("natural_log_exp_and_others")
            act.wait_ge(S["par_in"], 16)
            act.wait_ge(S["const0"], 6)
            a.activation(A[:], p("A_log"), ACT.Exp, bias=zero).then_inc(S["A_r"], 1)

            def square(hb, n):
                act.wait_ge(S["cen_r"], n + 1)
                a.activation(sq[:, hb, :], xm[:, hb, :], ACT.Square, bias=zero).then_inc(S["sq_r"], 1)

            def inverse_std(hb, n, b, bias):
                act.wait_ge(S["var_r"], n + 1)
                a.activation(sq[:, hb, :], bank[b][:], ACT.Ln, bias=bias).then_inc(S["ln_r"], 1)
                act.wait_ge(S["ln_r"], n + 1)
                a.activation(sq[:, hb, :], sq[:, hb, :], ACT.Exp, scale=-0.5, bias=zero).then_inc(S["rstd_r"], 1)

            def round_weights(c):
                act.wait_ge(S[f"w_in{c}"], 16)
                w, es = weight_chunk(c)
                a.activation(W_hi[w][:, es], stage(c), ACT.Copy).then_inc(S["w_hi"], 1)

            for hb in range(HALVES):
                square(hb, hb)
            for hb in range(HALVES):
                inverse_std(hb, hb, 2 + hb, eps_in)
            a.preload_act_table_set("silu_and_others")

            def copy_rank(gr):
                act.wait_ge(S["dtraw_r"], gr + 1)
                a.activation(dtr[0:2 * RANK, gr, :], bank[gr][0:2 * RANK, :], ACT.Copy).then_inc(S["dtr_r"], 1)

            def round_bc(gr):
                act.wait_ge(S["bc_r"], gr + 1)
                a.activation(BC[:, gr, :], bank[4 + gr][:], ACT.Copy).then_inc(S["bch_r"], 1)

            def magnitude(gr):
                act.wait_ge(S["dtp_r"], gr + 1)
                a.activation(dt[:, gr, :], bank[dt_bank(gr)][:], ACT.Abs, bias=zero).then_inc(S["abs_r"], 1)

            def softplus_z(gr):
                act.wait_ge(S["abs_r"], gr + 1)
                a.activation(dt[:, gr, :], dt[:, gr, :], ACT.Sigmoid, scale=-1.0, bias=mln2).then_inc(S["lz_r"], 1)

            def gate_z(gr):
                act.wait_ge(S["z_r"], gr + 1)
                a.activation(zs[:, gr, :], bank[gr][:], ACT.Silu, bias=zero).then_inc(S["zs_r"], 1)

            def present_tap(gr):
                act.wait_ge(S["xi_r"], gr + 1)
                cw = COLS["conv_w"][0] + TAPS - 1
                a.activation(y[:, gr, :], bank[4 + gr][:], ACT.Copy, scale=par[:, cw:cw + 1]).then_inc(S["tap0_r"], 1)

            def convolved(gr):
                hb, q = divmod(gr, PAIRS)
                act.wait_ge(S["conv_r"], (TAPS - 1) * PAIRS * hb + (TAPS - 2) * PAIRS + q + 1)
                a.activation(xc[:, gr, :], y[:, gr, :], ACT.Silu, bias=p("conv_b")).then_inc(S["xc_r"], 1)

            for c in (0, 1):
                round_weights(c)
            for gr in (0, 1):
                present_tap(gr)
            for gr in (0, 1):
                gate_z(gr)
            for c in (2, 3):
                round_weights(c)
            for gr in (2, 3):
                present_tap(gr)
            for gr in (0, 1):
                convolved(gr)
            for gr in (2, 3):
                gate_z(gr)
            act.wait_ge(S["const1"], 3)
            for gr in (0, 1):
                copy_rank(gr)
                round_bc(gr)
            for gr in (2, 3):
                convolved(gr)
            for gr in (0, 1):
                magnitude(gr)
            a.preload_act_table_set("sigmoid_and_others")
            softplus_z(0)
            softplus_z(1)
            for gr in (2, 3):
                copy_rank(gr)
                round_bc(gr)
            for gr in (2, 3):
                magnitude(gr)

            def copy_b(k):
                act.wait_ge(S["pB"], k + 1)
                if k >= 3:
                    act.wait_ge(S["u_r"], k - 2)
                a.activation(Bs[:, k % 3], bank[b_bank(k)][:], ACT.Copy).then_inc(S["Bs_r"], 1)

            def decay(k):
                if k >= 3:
                    act.wait_ge(S["scan_r"], 2 * (k - 2))
                s = k % NS
                a.activation(dA[:, k % 3], dt[:, k // NS, :], ACT.Exp, scale=A[:, s:s + 1], bias=zero)\
                    .then_inc(S["dA_r"], 1)

            def scan_step(k):
                if k + 2 < STEPS:
                    decay(k + 2)
                if k + 3 < STEPS:
                    copy_b(k + 3)

            for gr in (2, 3):
                softplus_z(gr)
            for k in range(3):
                copy_b(k)
            a.preload_act_table_set("natural_log_exp_and_others")
            act.wait_ge(S["A_r"], 2)
            act.wait_ge(S["w_lo"], CHUNKS_W - LAST_RESTS)
            act.wait_ge(S["dt_r"], 1)
            for k in range(2):
                decay(k)
            for k in range(SCAN0, SCAN1):
                if (k + 2) % NS == 0:
                    act.wait_ge(S["dt_r"], (k + 2) // NS + 1)
                scan_step(k)

            def back(hb, i):
                bk = BACK[hb]
                if i == 3:
                    square(hb, HALVES + 2 * hb)
                if i in (4, 8) and hb:
                    a.preload_act_table_set("natural_log_exp_and_others")
                if i == 4:
                    inverse_std(hb, HALVES + 2 * hb, bk[0], eps)
                if i == 7:
                    square(hb, HALVES + 2 * hb + 1)
                if i == 8:
                    inverse_std(hb, HALVES + 2 * hb + 1, bk[1], eps)
                if i in (4, 8) and hb:
                    a.preload_act_table_set("exp_and_others")
                if i == 9:
                    act.wait_ge(S["tn_r"], hb + 1)
                    a.activation(tn_hi[:, hb, :], tn[:, hb, :], ACT.Copy).then_inc(S["tnh_r"], 1)
                if i == 10:
                    act.wait_ge(S["dif_r"], hb + 1)
                    a.activation(e1[:], e1[:], ACT.Exp, bias=zero).then_inc(S["ex_r"], 1)
                if i == 12:
                    act.wait_ge(S["tr_r"], BLK * (hb + 1))
                    a.activation(CE[:, hb, :], bank[bk[1]][0:64, :], ACT.Copy).then_inc(S["ceh_r"], 1)

            def round_scaled(k):
                act.wait_ge(S["xs_r"], k + 1)
                if k >= 2:
                    act.wait_ge(S["up_r"], FH * (k - 1))
                a.activation(xs_hi[:, k % 2, :], xs, ACT.Copy).then_inc(S["xsh_r"], 1)

            def round_hidden(k, f):
                act.wait_ge(S["hid_r"], FH * k + f + 1)
                slot = FH * k + f
                if slot >= FH * E + 3:
                    act.wait_ge(S["yd_r"], slot - 2)
                a.activation(hid_hi[:, slot % 3], hid[k % 2][:, f, :], ACT.Copy).then_inc(S["hidh_r"], 1)

            def gate_tanh(k, f):
                act.wait_ge(S["g_r"], FH * k + f + 1)
                if k:
                    act.wait_ge(S["hid_r"], FH * (k - 1) + f + 1)
                a.activation(th[:, f, :], bank[GATE[f]][:], ACT.Tanh, scale=0.5, bias=zero).then_inc(S["th_r"], 1)

            for k in range(SCAN1, LEAD_END):
                back(0, BACK_ACT.get(k - BACK_STEP))
                if k == LEAD_END - 1:
                    round_scaled(0)
                scan_step(k)
            a.preload_act_table_set("exp_and_others")
            for k in range(HALVES * E):
                for f in range(FH):
                    gate_tanh(k, f)
                    j = beside(FH * k + f)
                    if j is not None and j < STEPS:
                        scan_step(j)
                    back(1, back_item(FH * k + f))
                    if down_in_parts(FH * k + f - 1):
                        round_hidden((FH * k + f - 1) // FH, (FH * k + f - 1) % FH)
                    if f == 0 and k + 1 < HALVES * E:
                        round_scaled(k + 1)
                    c = down_chunk(FH * k + f)
                    if c is not None:
                        act.wait_ge(S["acc_r"], acc_count(STEPS))
                        a.activation(Wd_hi[:, 2 * c:2 * c + 2], Wd[:, 2 * c:2 * c + 2], ACT.Copy)\
                            .then_inc(S["wd_hi"], 1)

        @block.vector
        def _(dve):
            v = nc.vector

            def centre(hb, n, b, src):
                dve.wait_ge(S["mean_r"], n + 1)
                v.tensor_tensor(xm[:, hb, :], src, bank[b][:], ALU.subtract).then_inc(S["cen_r"], 1)

            def scale(hb, n, name="norm_r"):
                dve.wait_ge(S["rstd_r"], n + 1)
                v.tensor_tensor(xm[:, hb, :], xm[:, hb, :], sq[:, hb, :], ALU.mult).then_inc(S[name], 1)

            for hb in range(HALVES):
                centre(hb, hb, hb, X[:, hb, :])
            dve.wait_ge(S["sel1"], 4)
            v.tensor_copy(sel[:].rearrange("r s (j d) -> r s j d", j=2),
                          unit.rearrange("r (j s o) -> r s j o", j=2, o=1).broadcast_to([P, NS, 2, DI]))\
                .then_inc(S["sel_r"], 1)
            v.tensor_scalar(sel_e[:], unit[0:64, 0:E], 0.5, None, ALU.mult).then_inc(S["sele_r"], 1)
            dve.wait_ge(S["A_r"], 1)
            v.tensor_scalar(A[:], A[:], -1.0, None, ALU.mult).then_inc(S["A_r"], 1)
            for hb in range(HALVES):
                scale(hb, hb)
            dve.wait_ge(S["par_in"], 16)
            for hb in range(HALVES):
                dve.wait_ge(S["norm_r"], hb + 1)
                v.tensor_scalar(chk[:, hb, :], xm[:, hb, :], p("norm_g"), p("norm_b"), ALU.mult, ALU.add)\
                    .then_inc(S["chk_r"], 1)
            cw = COLS["conv_w"][0]
            for hb in range(HALVES):
                for tap in range(1, TAPS):
                    for gr in range(PAIRS * hb, PAIRS * (hb + 1)):
                        w = par[:, cw + TAPS - 1 - tap:cw + TAPS - tap]
                        src = bank[4 + gr][:].rearrange("p (b t) -> p b t", t=T)[:, :, 0:T - tap]
                        dst = y[:, gr, :].rearrange("p (b t) -> p b t", t=T)[:, :, tap:T]
                        if tap == 1:
                            dve.wait_ge(S["tap0_r"], gr + 1)
                        else:
                            dve.wait_ge(S["conv_r"], ((TAPS - 1) * hb + tap - 2) * PAIRS + gr % PAIRS + 1)
                        v.scalar_tensor_tensor(dst, src, w, dst, ALU.mult, ALU.add).then_inc(S["conv_r"], 1)

            def bc_rest(gr):
                dve.wait_ge(S["bch_r"], gr + 1)
                v.scalar_tensor_tensor(BC[:, gr, :], BC[:, gr, :].bitcast(F32), rest_row, bank[4 + gr][:],
                                       ALU.mult, ALU.add).then_inc(S["bcl_r"], 1)

            def square_z(gr):
                dve.wait_ge(S["lz_r"], gr + 1)
                v.tensor_tensor(lw[:, gr, :], dt[:, gr, :], dt[:, gr, :], ALU.mult).then_inc(S["lw_r"], 1)

            def softplus(gr, i):
                if i == 0:
                    dve.wait_ge(S["lw_r"], gr + 1)
                    v.tensor_scalar(lr[:, gr, :], lw[:, gr, :], LOG1P[4], LOG1P[3], ALU.mult, ALU.add)\
                        .then_inc(S["lq_r"], 1)
                elif i < 4:
                    dve.wait_ge(S["lq_r"], 4 * gr + i)
                    v.scalar_tensor_tensor(lr[:, gr, :], lr[:, gr, :], 0.0 if i == 1 else LOG1P[4 - i], lw[:, gr, :],
                                           ALU.add, ALU.mult).then_inc(S["lq_r"], 1)
                elif i == 4:
                    dve.wait_ge(S["lq_r"], 4 * gr + 4)
                    v.scalar_tensor_tensor(lr[:, gr, :], lr[:, gr, :], LOG1P[0], dt[:, gr, :], ALU.add, ALU.mult)\
                        .then_inc(S["lp_r"], 1)
                else:
                    dve.wait_ge(S["lp_r"], gr + 1)
                    v.scalar_tensor_tensor(dt[:, gr, :], bank[dt_bank(gr)][:], 0.0, lr[:, gr, :], ALU.max, ALU.add)\
                        .then_inc(S["dt_r"], 1)

            dve.wait_ge(S["rest0"], 3)

            def round_weights(c):
                dve.wait_ge(S[f"w_in{c}"], 16)
                w, es = weight_chunk(c)
                v.tensor_copy(W_hi[w][:, es], stage(c)).then_inc(S["w_hi2"], 1)

            bc_rest(0)
            for c in range(ACT_ROUNDS, ACT_ROUNDS + 4):
                round_weights(c)
            bc_rest(1)
            for c in range(ACT_ROUNDS + 4, CHUNKS_W - LAST_RESTS):
                round_weights(c)
            square_z(0)
            for i in range(6):
                softplus(0, i)
                if i == 2:
                    bc_rest(2)
            bc_rest(3)
            for c in range(CHUNKS_W - LAST_RESTS, CHUNKS_W):
                round_weights(c)
            for gr in range(1, GROUPS):
                square_z(gr)
            dve.wait_ge(S["w_lo"], CHUNKS_W - LAST_RESTS)

            def scan(k):
                dve.wait_ge(S["dA_r"], k + 1)
                dve.wait_ge(S["u_r"], k + 1)
                if k >= 3:
                    dve.wait_ge(S["hc_r"], k - 2)
                for b in range(2):
                    t = slice(b * T, (b + 1) * T)
                    v.tensor_tensor_scan(h[:, k % 3, t], dA[:, k % 3, t], u[:, k % 3, t], 0.0,
                                         ALU.mult, ALU.add).then_inc(S["scan_r"], 1)

            def weigh(k):
                dve.wait_ge(S["pC"], k + 1)
                dve.wait_ge(S["scan_r"], 2 * (k + 1))
                if k >= 3:
                    dve.wait_ge(S["red_r"], min(k - 2, POOL0))
                if k - 3 > POOL0:
                    dve.wait_ge(S["acc_r"], acc_count(k - 2))
                dst = y[:, k // NS, :] if k == POOL0 else hc[:, k % 3]
                v.tensor_tensor(dst, h[:, k % 3], bank[c_bank(k)][:], ALU.mult).then_inc(S["hc_r"], 1)

            def finish_group(gr):
                if gr < GROUPS - 1:
                    dve.wait_ge(S["red_r"], NS * (gr + 1))
                    total = bank[STATE_SUM[gr]][:]
                else:
                    dve.wait_ge(S["acc_r"], acc_count(STEPS))
                    total = y[:, gr, :]
                v.scalar_tensor_tensor(y[:, gr, :], xc[:, gr, :], p("D"), total, ALU.mult, ALU.add)\
                    .then_inc(S["yg_r"], 1)
                dve.wait_ge(S["yg_r"], gr + 1)
                v.tensor_tensor(y[:, gr, :], y[:, gr, :], zs[:, gr, :], ALU.mult).then_inc(S["y_r"], 1)

            def back(hb, i):
                bk = BACK[hb]
                if i == 0:
                    finish_group(PAIRS * hb + 1)
                if i == 1:
                    dve.wait_ge(S["op_r"], hb + 1)
                    v.scalar_tensor_tensor(chk[:, hb, :], chk[:, hb, :], p("skip"), bank[bk[0]][:], ALU.mult, ALU.add)\
                        .then_inc(S["y2_r"], 1)
                if i == 2:
                    dve.wait_ge(S["w_lo"], CHUNKS_W)
                    centre(hb, HALVES + 2 * hb, bk[1], chk[:, hb, :])
                if i == 4:
                    scale(hb, HALVES + 2 * hb)
                    dve.wait_ge(S["norm_r"], HALVES + hb + 1)
                    v.tensor_scalar(chk[:, hb, :], xm[:, hb, :], p("norm_g"), p("norm_b"), ALU.mult, ALU.add)\
                        .then_inc(S["y3_r"], 1)
                if i == 5:
                    dve.wait_ge(S["pj_r"], hb + 1)
                    v.scalar_tensor_tensor(X[:, hb, :], bank[bk[1]][:], p("proj_b"), X[:, hb, :], ALU.add, ALU.add)\
                        .then_inc(S["x1_r"], 1)
                if i == 6:
                    centre(hb, HALVES + 2 * hb + 1, bk[0], X[:, hb, :])
                if i == 8:
                    scale(hb, HALVES + 2 * hb + 1, "tn_r")
                if i == 9:
                    dve.wait_ge(S["tnh_r"], hb + 1)
                    v.tensor_tensor(tn_lo[:, hb, :], tn[:, hb, :], tn_hi[:, hb, :].bitcast(F32), ALU.subtract)\
                        .then_inc(S["tnl_r"], 1)
                if i == 9:
                    dve.wait_ge(S["lg_r"], hb + 1)
                    v.tensor_copy(L[hb].rearrange("p b e -> p (b e)"), bank[bk[0]][:, 0:BLK * E]).then_inc(S["L_r"], 1)
                    dve.wait_ge(S["L_r"], hb + 1)
                    for b in range(BLK):
                        v.max(top[:, b, :], L[hb][:, b, :]).then_inc(S["top_r"], 1)
                    for b in range(BLK):
                        dve.wait_ge(S["top_r"], BLK * hb + b + 1)
                        v.max_index(topi[:, b, :], top[:, b, :], L[hb][:, b, :]).then_inc(S["topi_r"], 1)
                    v.tensor_tensor(e1[:], top[:, :, 1:2], top[:, :, 0:1], ALU.subtract).then_inc(S["dif_r"], 1)
                    dve.wait_ge(S["topi_r"], BLK * (hb + 1))
                    v.tensor_copy(topf[:], topi[:, :, 0:2]).then_inc(S["topf_r"], 1)
                if i == 10:
                    dve.wait_ge(S["topf_r"], hb + 1)
                    for j in range(2):
                        v.tensor_tensor(oh[hb][:, j], iota_e[:], topf[:, :, j:j + 1].broadcast_to([P, BLK, E]),
                                        ALU.is_equal).then_inc(S["eq_r"], 1)
                    dve.wait_ge(S["ex_r"], hb + 1)
                    v.tensor_scalar(w01[:, :, 0:1], e1[:], 1.0, None, ALU.add).then_inc(S["sum_r"], 1)
                    dve.wait_ge(S["sum_r"], hb + 1)
                    v.reciprocal(w01[:, :, 0:1], w01[:, :, 0:1]).then_inc(S["w0_r"], 1)
                    dve.wait_ge(S["w0_r"], hb + 1)
                    v.tensor_tensor(w01[:, :, 1:2], e1[:], w01[:, :, 0:1], ALU.mult).then_inc(S["w1_r"], 1)
                    dve.wait_ge(S["w1_r"], hb + 1)
                    for j in range(2):
                        dve.wait_ge(S["eq_r"], 2 * hb + j + 1)
                        w = w01[:, :, j:j + 1].broadcast_to([P, BLK, E])
                        v.tensor_tensor(oh[hb][:, j], oh[hb][:, j], w, ALU.mult).then_inc(S["ow_r"], 1)
                    dve.wait_ge(S["ow_r"], 2 * hb + 2)
                    for part in range(2):
                        v.tensor_tensor(cpad[:, :, 32 * part:32 * part + E], oh[hb][:, 0], oh[hb][:, 1], ALU.add)\
                            .then_inc(S["ce_r"], 1)
                if i == 12:
                    dve.wait_ge(S["ceh_r"], hb + 1)
                    v.tensor_tensor(CE[32:64, hb, :], bank[bk[1]][32:64, :], CE[32:64, hb, :].bitcast(F32),
                                    ALU.subtract).then_inc(S["cel_r"], 1)

            def scale_tokens(k):
                dve.wait_ge(S["ceb_r"], k + 1)
                if k:
                    dve.wait_ge(S["xsl_r"], k)
                v.tensor_tensor(xs, tn[:, k // E, :], bank[SPREAD][:], ALU.mult).then_inc(S["xs_r"], 1)

            def gate(k, f):
                dve.wait_ge(S["th_r"], FH * k + f + 1)
                v.scalar_tensor_tensor(th[:, f, :], th[:, f, :], 1.0, bank[GATE[f]][:], ALU.add, ALU.mult)\
                    .then_inc(S["m_r"], 1)

            def result(hb):
                dve.wait_ge(S["yd_r"], (hb + 1) * E * FH)
                v.tensor_tensor(X[:, hb, :], X[:, hb, :], bank[YSUM][:], ALU.add).then_inc(S["res_r"], 1)

            def hidden(k, f):
                dve.wait_ge(S["up_r"], FH * k + f + 1)
                dve.wait_ge(S["m_r"], FH * k + f + 1)
                if k >= E + 2:
                    dve.wait_ge(S["hidl_r"], FH * (k - 2 - E) + f + 1)
                elif k >= 2:
                    dve.wait_ge(S["yd_r"], FH * (k - 2) + f + 1)
                v.tensor_tensor(hid[k % 2][:, f, :], th[:, f, :], bank[UP[f]][:], ALU.mult).then_inc(S["hid_r"], 1)

            for k in range(SCAN0, SCAN1):
                scan(k)
                if k:
                    weigh(k - 1)
                if k // 6 + 1 < GROUPS:
                    softplus(k // 6 + 1, k % 6)
                if k == NS + 3:
                    finish_group(0)
            for k in range(SCAN1, LEAD_END):
                scan(k)
                weigh(k - 1)
                back(0, BACK_DVE.get(k - BACK_STEP))
                if k == LEAD_END - 2:
                    scale_tokens(0)
            weigh(LEAD_END - 1)
            for k in range(HALVES * E):
                for f in range(FH):
                    if f == 0 and k + 1 < HALVES * E:
                        scale_tokens(k + 1)
                    gate(k, f)
                    j = beside(FH * k + f)
                    if j is not None and j < STEPS:
                        scan(j)
                    hidden(k, f)
                    if j is not None and j > LEAD_END:
                        weigh(j - 1)
                    back(1, back_item(FH * k + f))
                    if k == 0 and f == 0:
                        finish_group(2)
                if k == E:
                    result(0)
            result(1)

        @block.tensor
        def _(pe):
            t = nc.tensor
            pe.wait_ge(S["const0"], 2)

            def mm(o, w, r, name, start=True, stop=True):
                return t.matmul(o, w, r, start=start, stop=stop).then_inc(S[name], 1)

            def mean(b, src):
                mm(bank[b][:], mean_w[:], src, "mean_r")

            def variance(hb, n, b, w):
                pe.wait_ge(S["sq_r"], n + 1)
                mm(bank[b][:], w, sq[:, hb, :], "var_r")

            def keep_warm(count, b=7):
                for _ in range(count):
                    t.matmul(bank[b][:, 0:P], mean_w[:], mean_w[:], start=True, stop=True)

            keep_warm(8)
            for hb in range(HALVES):
                pe.wait_ge(S[f"x_in{hb}"], 16)
                mean(hb, X[:, hb, :])
            for hb in range(HALVES):
                variance(hb, hb, 2 + hb, var_in_w)
            keep_warm(12)
            pe.wait_ge(S["par_in"], 16)
            for hb in range(HALVES):
                pe.wait_ge(S["chk_r"], hb + 1)
                for q in range(PAIRS):
                    rows = slice(64 * q, 64 * q + 64)
                    mm(bank[4 + 2 * hb + q][:], p("in_x")[rows], chk[rows, hb, :], "xi_r")
                if hb == 0:
                    pe.wait_ge(S["cen_r"], HALVES)
                    pe.wait_ge(S["ln_r"], HALVES)
                for q in range(PAIRS):
                    rows = slice(64 * q, 64 * q + 64)
                    mm(bank[2 * hb + q][:], p("in_z")[rows], chk[rows, hb, :], "z_r")

            def project_dt(gr):
                pe.wait_ge(S["dtr_r"], gr + 1)
                if gr:
                    pe.wait_ge(S["bcl_r"], gr)
                mm(bank[dt_bank(gr)][:], p("dt_out")[0:DTK], dtr[:, gr, :], "dtp_r")

            for hb in range(HALVES):
                for gr in range(PAIRS * hb, PAIRS * (hb + 1)):
                    pe.wait_ge(S["xc_r"], gr + 1)
                    pe.wait_ge(S["zs_r"], gr + 1)
                    mm(bank[gr][0:2 * RANK, :], p("dt_in"), xc[:, gr, :], "dtraw_r")
                    mm(bank[4 + gr][:], p("bc"), xc[:, gr, :], "bc_r")
                for gr in range(PAIRS * hb, PAIRS * (hb + 1)):
                    project_dt(gr)
            pe.wait_ge(S["sel_r"], 1)
            pe.wait_ge(S["ident_r"], 1)
            pe.wait_ge(S["bcl_r"], 1)

            def sum_state(k):
                gr, s = divmod(k, NS)
                if k == 2 * NS:
                    pe.wait_ge(S["yg_r"], 2)
                elif k == NS:
                    pe.wait_ge(S["dt_r"], GROUPS)
                pe.wait_ge(S["hc_r"], k + 1)
                mm(bank[STATE_SUM[gr]][:], ident[:], hc[:, k % 3], "red_r", s == 0, s == NS - 1)

            def spread_b(k, idle=0):
                if before(b_bank, k):
                    pe.wait_ge(S["Bs_r"], before(b_bank, k))
                keep_warm(idle, b_bank(k))
                mm(bank[b_bank(k)][:], sel[0:64, k % NS, :], BC[0:64, k // NS, :], "pB")

            def spread_c(k):
                if before(c_bank, k):
                    pe.wait_ge(S["hc_r"], before(c_bank, k))
                mm(bank[c_bank(k)][:], sel[64:128, k % NS, :], BC[64:128, k // NS, :], "pC")

            pe.wait_ge(S["sele_r"], 1)
            for k in range(3):
                spread_b(k)
            spread_c(0)
            pe.wait_ge(S["bcl_r"], GROUPS)
            keep_warm(8)
            pe.wait_ge(S["dt_r"], 1)
            for k in range(SCAN0, SCAN1):
                spread_b(k + 3, 2 if k < WARM_STEPS else 0)
                if k >= 2:
                    sum_state(k - 2)
                if k + 1 < SCAN1:
                    spread_c(k + 1)

            def back(hb, i):
                bk = BACK[hb]
                if i == 1:
                    for q in range(PAIRS):
                        pe.wait_ge(S["y_r"], 2 * hb + q + 1)
                        o = t.matmul(bank[bk[0]][64 * q:64 * q + 64, :], p("out"), y[:, 2 * hb + q, :],
                                     start=True, stop=True)
                    o.then_inc(S["op_r"], 1)
                if i == 2:
                    pe.wait_ge(S["y2_r"], hb + 1)
                    mean(bk[1], chk[:, hb, :])
                if i == 3:
                    variance(hb, HALVES + 2 * hb, bk[0], mean_w[:])
                if i == 5:
                    pe.wait_ge(S["y3_r"], hb + 1)
                    mm(bank[bk[1]][:], p("proj"), chk[:, hb, :], "pj_r")
                if i == 6:
                    pe.wait_ge(S["x1_r"], hb + 1)
                    mean(bk[0], X[:, hb, :])
                if i == 7:
                    variance(hb, HALVES + 2 * hb + 1, bk[1], mean_w[:])
                if i == 9:
                    pe.wait_ge(S["tn_r"], hb + 1)
                    for b in range(BLK):
                        o = t.matmul(bank[bk[0]][:, b * E:(b + 1) * E], tn[:, hb, b * P:(b + 1) * P], p("router"),
                                     start=True, stop=True)
                    o.then_inc(S["lg_r"], 1)
                if i == 11:
                    pe.wait_ge(S["ce_r"], 2 * (hb + 1))
                    for b in range(BLK):
                        t.transpose(bank[bk[1]][0:64, b * P:(b + 1) * P], cpad[:, b, :], ident[:])\
                            .then_inc(S["tr_r"], 1)

            def spread_gate(k):
                pe.wait_ge(S["cel_r"], k // E + 1)
                if k:
                    pe.wait_ge(S["xs_r"], k)
                mm(bank[SPREAD][:], sel_e[:, k % E:k % E + 1].broadcast_to([P // 2, P]), CE[:, k // E, :], "ceb_r")

            def product(b, w_hi, w_lo, hi, lo, name, first=True, last=True):
                t.matmul(bank[b][:], w_hi, hi, start=first, stop=False)
                t.matmul(bank[b][:], w_hi, lo, start=False, stop=False)
                mm(bank[b][:], w_lo, hi, name, False, last)

            def project(b, w, k, f, hi, lo, name):
                ws = slice(f * P, (f + 1) * P)
                product(b, W_hi[w][:, k % E, ws], W_lo[w][:, k % E, ws], hi, lo, name)

            def down(k, f):
                e = k % E
                if down_in_parts(FH * k + f):
                    pe.wait_ge(S["hidl_r"], FH * (k - E) + f + 1)
                else:
                    pe.wait_ge(S["hid_r"], FH * k + f + 1)
                i = (FH * k + f) % 3
                first, last = e == 0 and f == 0, e == E - 1 and f == FH - 1
                if first:
                    if k:
                        pe.wait_ge(S["res_r"], k // E)
                        pe.wait_ge(S["wd_lo"], E // 2)
                    else:
                        pe.wait_ge(S["yg_r"], 3)
                if not down_in_parts(FH * k + f):
                    mm(bank[YSUM][:], Wd[:, e, f, :], hid[k % 2][:, f, :], "yd_r", first, last)
                else:
                    product(YSUM, Wd_hi[:, e, f, :], Wd_lo[:, e, f, :], hid_hi[:, i], hid_lo[:, i], "yd_r", first, last)

            for k in range(SCAN1, LEAD_END):
                if k == LEAD_END - 2:
                    spread_gate(0)
                spread_b(k + 3)
                spread_c(k)
                if k - 2 < POOL0:
                    sum_state(k - 2)
                back(0, BACK_PE.get(k - BACK_STEP))
            for k in range(LEAD_END - 2, POOL0):
                sum_state(k)
            pe.wait_ge(S["wd_in"], 16)
            pe.wait_ge(S["w_lo"], CHUNKS_W)
            for k in range(HALVES * E):
                hb = k // E
                for f in range(FH):
                    slot = FH * k + f
                    if f == 0:
                        if k + 1 < HALVES * E:
                            spread_gate(k + 1)
                        pe.wait_ge(S["tnl_r"], hb + 1)
                    if slot == 1:
                        pe.wait_ge(S["hc_r"], LEAD_END)
                        pe.wait_ge(S["Bs_r"], LEAD_END)
                    if slot >= FH:
                        pe.wait_ge(S["m_r"], slot - 1)
                    project(GATE[f], 0, k, f, tn_hi[:, hb, :], tn_lo[:, hb, :], "g_r")
                    if back_item(slot - 1) in LATE:
                        back(1, back_item(slot - 1))
                    j = beside(slot)
                    if j is not None and j + 3 < STEPS:
                        spread_b(j + 3)
                    if f == 0:
                        pe.wait_ge(S["xsl_r"], k + 1)
                    if slot >= FH:
                        pe.wait_ge(S["hid_r"], slot - 1)
                    project(UP[f], 1, k, f, xs_hi[:, k % 2, :], xs_lo[:, k % 2, :], "up_r")
                    if 1 <= k <= E:
                        down(k - 1, f)
                    elif slot - 3 >= FH * E:
                        down((slot - 3) // FH, (slot - 3) % FH)
                    if j is not None and j > LEAD_END:
                        spread_c(j - 1)
                    if back_item(slot) not in LATE:
                        back(1, back_item(slot))
            for slot in range(FH * HALVES * E - 3, FH * HALVES * E):
                down(slot // FH, slot % FH)


def kernel(**inputs):
    import concourse.bacc as bacc
    from concourse.bass_utils import run_bass_kernel_spmd as run

    a = {k.removeprefix("L0_"): np.asarray(v) for k, v in inputs.items()}
    par = np.zeros((P, NPACK), np.float32)

    def put(name, m, row=0, col=0):
        c0 = COLS[name][0] + col
        par[row:row + m.shape[0], c0:c0 + m.shape[1]] = m

    put("norm_g", a["conv_norm_g"][:, None])
    put("norm_b", a["conv_norm_b"][:, None])
    put("proj_b", a["conv_proj_b"][:, None])
    put("skip", np.broadcast_to(a["conv_skip_scale"][:, None], (P, 1)))
    put("proj", a["conv_proj_w"].T)
    put("router", a["ffn_router_w"].T)
    for j in range(2):
        for name, key in (("conv_b", "conv_conv_b"), ("D", "conv_D_param")):
            put(name, a[key][:, None], DI * j)
        put("conv_w", a["conv_conv_w"], DI * j)
        put("A_log", a["conv_A_log"], DI * j)
        put("dt_in", a["conv_x_proj_w"].T[:, 0:RANK], DI * j, RANK * j)
        put("dt_out", a["conv_dt_proj_w"].T, RANK * j, DI * j)
        put("dt_out", a["conv_dt_proj_b"][None, :], 2 * RANK, DI * j)
        put("out", a["conv_out_proj_w"].T, DI * j, DM * j)
        for part in range(2):
            for i in range(2):
                rows = a["conv_x_proj_w"].T[:, RANK + NS * i:RANK + NS * (i + 1)]
                put("bc", rows, DI * j, 64 * i + 32 * part + NS * j)
    for q in range(CHUNKS):
        put("in_x", a["conv_in_proj_w"].T[:, 0:DI], DM * q, DI * (q % 2))
        put("in_z", a["conv_in_proj_w"].T[:, DI:2 * DI], DM * q, DI * (q % 2))
    arrays = {"x": np.ascontiguousarray(a["x"].reshape(BATCH, C, T)), "params": par, "gate_w": a["ffn_gate_w"],
              "up_w": a["ffn_up_w"], "down_w": a["ffn_down_w"]}

    nc = bacc.Bacc("TRN2", target_bir_lowering=False, num_devices=1)
    args = [nc.dram_tensor(k, v.shape, F32, kind="ExternalInput").ap() for k, v in arrays.items()]
    out = nc.dram_tensor("out", (BATCH, C, T), F32, kind="ExternalOutput").ap()
    build(nc, *args, out)
    r = run(nc, [arrays], core_ids=[0])
    return r.results[0]["out"].reshape(BATCH, C, 16, 16)
```
